# Optimizing a Trainium2 kernel written in Bass

```python
import numpy as np
import jax
import jax.numpy as jnp

def _softmax(x, axis=-1):
    return jax.nn.softmax(x, axis=axis)

def _gelu(x):
    return jax.nn.gelu(x, approximate=True)

def _silu(x):
    return jax.nn.silu(x)

def _sigmoid(x):
    return jax.nn.sigmoid(x)

def _layernorm(x, axis=-1, eps=1e-05):
    m = jnp.mean(x, axis=axis, keepdims=True)
    v = jnp.var(x, axis=axis, keepdims=True)
    return (x - m) / jnp.sqrt(v + eps)

def _scatter_add(tgt, idx, src, axis=0):
    return tgt.at[idx].add(src)

def _segment_sum(src, seg, n):
    return jax.ops.segment_sum(src, seg, n)
kernel_name = 'mk_adaln_ffn_d1_seqx_r8_8ae90f'

def setup_inputs(seed: int=0):
    np.random.seed(seed)
    _w = jnp.asarray

    def _rec_inputs():
        import jax
        import jax.numpy as jnp
        _rk = jax.random.key(seed)
        x = -7.109e-05 + 0.9999 * jax.random.normal(jax.random.fold_in(_rk, 1), (32, 32, 256), jnp.float32)
        _lenS = 32 - jax.random.randint(jax.random.fold_in(_rk, 7), (32,), 0, max(1, 32 // 4) + 1, jnp.int32)
        _lenS2 = 32 - jax.random.randint(jax.random.fold_in(_rk, 8), (32,), 0, max(1, 32 // 4) + 1, jnp.int32)
        itok_B_0_6 = jax.random.randint(jax.random.fold_in(_rk, 11), (32,), 0, 7, jnp.int32)
        return (x, itok_B_0_6)
    x, itok_B_0_6 = _rec_inputs()

    def _L0_cond_setup():
        import jax, jax.numpy as jnp
        import numpy as np
        B, T, D_IN, D_OUT = (16, 256, 256, 256)
        N_ADAPTERS, RANK = (8, 16)
        key = jax.random.key(seed)
        k_x, k_w, k_a, k_b, k_s, k_idx = jax.random.split(key, 6)
        x = jax.random.normal(k_x, (B, T, D_IN), dtype=jnp.float32)
        W = jax.random.normal(k_w, (D_OUT, D_IN), dtype=jnp.float32) * (1.0 / np.sqrt(D_IN))
        A = jax.random.normal(k_a, (N_ADAPTERS, RANK, D_IN), dtype=jnp.float32) * 0.02
        Bm = jax.random.normal(k_b, (N_ADAPTERS, D_OUT, RANK), dtype=jnp.float32) * 0.02
        scalings = jnp.ones((N_ADAPTERS,), dtype=jnp.float32)
        adapter_idx = jax.random.randint(k_idx, (B,), 0, N_ADAPTERS, dtype=jnp.int32)
        return {'x': x, 'W': W, 'A': A, 'Bm': Bm, 'scalings': scalings, 'adapter_idx': adapter_idx}
    _L0_cond_all = _L0_cond_setup()
    _L0_cond_in = {k: v for k, v in _L0_cond_all.items() if k in ('W', 'A', 'Bm', 'scalings')}
    del _L0_cond_all

    def _L0_ffn_setup():
        import jax, jax.numpy as jnp
        import numpy as np
        B, S, H = (2, 256, 256)
        E, K = (16, 4)
        I_MOE, I_SH = (176, 704)
        key = jax.random.key(seed)
        ks = jax.random.split(key, 9)

        def w(k, shape, fan_in):
            return jax.random.normal(k, shape, jnp.float32) * fan_in ** (-0.5)
        return {'hidden_states': jax.random.normal(ks[0], (B, S, H), jnp.float32), 'router_w': w(ks[1], (E, H), H), 'w_gate': w(ks[2], (E, H, I_MOE), H), 'w_up': w(ks[3], (E, H, I_MOE), H), 'w_down': w(ks[4], (E, I_MOE, H), I_MOE), 'sh_gate': w(ks[5], (H, I_SH), H), 'sh_up': w(ks[6], (H, I_SH), H), 'sh_down': w(ks[7], (I_SH, H), I_SH), 'sh_gate_w': w(ks[8], (H, 1), H)}
    _L0_ffn_all = _L0_ffn_setup()
    _L0_ffn_in = {k: v for k, v in _L0_ffn_all.items() if k in ('router_w', 'w_gate', 'w_up', 'w_down', 'sh_gate', 'sh_up', 'sh_down', 'sh_gate_w')}
    del _L0_ffn_all
    return {'x': x, 'itok_B_0_6': itok_B_0_6, 'L0_cond_W': _L0_cond_in['W'], 'L0_cond_A': _L0_cond_in['A'], 'L0_cond_Bm': _L0_cond_in['Bm'], 'L0_cond_scalings': _L0_cond_in['scalings'], 'L0_ffn_router_w': _L0_ffn_in['router_w'], 'L0_ffn_w_gate': _L0_ffn_in['w_gate'], 'L0_ffn_w_up': _L0_ffn_in['w_up'], 'L0_ffn_w_down': _L0_ffn_in['w_down'], 'L0_ffn_sh_gate': _L0_ffn_in['sh_gate'], 'L0_ffn_sh_up': _L0_ffn_in['sh_up'], 'L0_ffn_sh_down': _L0_ffn_in['sh_down'], 'L0_ffn_sh_gate_w': _L0_ffn_in['sh_gate_w']}

def reference(x, itok_B_0_6, L0_cond_W, L0_cond_A, L0_cond_Bm, L0_cond_scalings, L0_ffn_router_w, L0_ffn_w_gate, L0_ffn_w_up, L0_ffn_w_down, L0_ffn_sh_gate, L0_ffn_sh_up, L0_ffn_sh_down, L0_ffn_sh_gate_w):
    import jax
    import jax.numpy as jnp

    def _L0_cond_ref(x, W, A, Bm, scalings, adapter_idx):
        import jax, jax.numpy as jnp
        import numpy as np
        B, T, D_IN, D_OUT = (16, 256, 256, 256)
        N_ADAPTERS, RANK = (8, 16)
        H = jnp.einsum('btd,od->bto', x, W)
        A_b = A[adapter_idx]
        B_b = Bm[adapter_idx]
        s_b = scalings[adapter_idx]
        xa = jnp.einsum('btd,brd->btr', x, A_b)
        delta = jnp.einsum('btr,bor->bto', xa, B_b)
        delta = jax.lax.stop_gradient(delta * s_b[:, None, None])
        return H + delta

    def _L0_ffn_ref(hidden_states, router_w, w_gate, w_up, w_down, sh_gate, sh_up, sh_down, sh_gate_w):
        import jax, jax.numpy as jnp
        import numpy as np
        B, S, H = (2, 256, 256)
        E, K = (16, 4)
        I_MOE, I_SH = (176, 704)
        orig = hidden_states.shape
        h = hidden_states.reshape(-1, orig[-1])
        N = h.shape[0]
        logits = h @ router_w.T
        probs = jax.nn.softmax(logits.astype(jnp.float32), axis=-1)
        top_vals, top_idx = jax.lax.top_k(probs, K)
        top_vals = top_vals / jnp.maximum(top_vals.sum(-1, keepdims=True), 1e-09)
        top_vals = top_vals.astype(h.dtype)
        comb = jnp.zeros((N, E), h.dtype).at[jnp.arange(N)[:, None], top_idx].add(top_vals)
        g = jnp.einsum('nh,ehi->eni', h, w_gate)
        u = jnp.einsum('nh,ehi->eni', h, w_up)
        y = jnp.einsum('eni,eih->enh', jax.nn.silu(g) * u, w_down)
        routed = jnp.einsum('enh,ne->nh', y, comb)
        shared = jax.nn.silu(h @ sh_gate) * (h @ sh_up) @ sh_down
        sg = jax.nn.sigmoid(h @ sh_gate_w)
        return (routed + sg * shared).reshape(orig)
    x = x + _L0_ffn_ref(_L0_cond_ref(x, L0_cond_W, L0_cond_A, L0_cond_Bm, L0_cond_scalings, itok_B_0_6), L0_ffn_router_w, L0_ffn_w_gate, L0_ffn_w_up, L0_ffn_w_down, L0_ffn_sh_gate, L0_ffn_sh_up, L0_ffn_sh_down, L0_ffn_sh_gate_w)
    return x

_drawn_inputs = setup_inputs


def setup_inputs(seed=0):
    import zlib

    import numpy as np

    out = dict(_drawn_inputs(seed))
    spreads = {'L0_cond_scalings': (1.0, 0.6)}
    factors = {}
    for name, (base, spread) in spreads.items():
        noise = np.random.default_rng([zlib.crc32(name.encode()), seed]).standard_normal(out[name].shape)
        drawn = base * np.exp(spread * noise) if base else spread * noise
        out[name] = jnp.asarray(drawn.astype(out[name].dtype))
    for name, factor in factors.items():
        out[name] = (out[name] * factor).astype(out[name].dtype)
    return out
```

```python
from contextlib import ExitStack

import concourse.bass as bass
from concourse import mybir

F32 = mybir.dt.float32
F32R = mybir.dt.float32r
I32 = mybir.dt.int32
U32 = mybir.dt.uint32
ALU = mybir.AluOpType
ACT = mybir.ActivationFunctionType
AX_X = mybir.AxisListType.X

P = 128
HALF = 512
TOP_K = 4


def adaln_moe_ffn(nc, x, adapter_idx, cond_w, cond_a, cond_b, scalings, router_w, w_gate, w_up,
                  w_down, sh_gate, sh_up, sh_down, sh_gate_w, out):
    B, T, D = x.shape
    N = B * T
    NT = N // P
    KD = D // P
    NH = N // HALF
    TPH = HALF // P
    NA, RANK, _ = cond_a.shape
    E, _, I = w_gate.shape
    IS = sh_gate.shape[1]
    SF = IS // P
    SR = IS - SF * P
    RC = E * I // P
    FIRST_ROUTED = SF + 1
    CHUNKS = SF + 1 + RC
    GRAIN = 16
    REP = I // GRAIN
    LOADS = 2
    EL, CL = E // LOADS, RC // LOADS
    assert NA * RANK == P and 2 * SR == P and E * I == RC * P and NH == 2 and KD == 2
    assert I % GRAIN == 0 and RC % 2 == 0 and FIRST_ROUTED % 2 == 0 and EL * I == CL * P
    BH = B // NH

    x_tok = x.rearrange("b t d -> (b t) d").rearrange("(n p) d -> p n d", p=P)
    out_tok = out.rearrange("b t d -> (b t) d").rearrange("(n p) d -> p n d", p=P)
    comb_rows = nc.dram_tensor("comb_rows", [E * REP, N], F32, kind="Internal").ap()

    with ExitStack() as ctx:
        def sb(name, shape, dt=F32):
            return ctx.enter_context(nc.sbuf_tensor(name, shape, dt))

        def sem(name):
            return ctx.enter_context(nc.semaphore(name))

        x_sb = sb("x_sb", [P, NT, D])
        cond_w_sb = sb("cond_w_sb", [P, KD, D])
        cond_a_sb = sb("cond_a_sb", [P, D])
        cond_b_sb = sb("cond_b_sb", [P, KD, NA, RANK])
        router_sb = sb("router_sb", [E, D])
        shw_sb = sb("shw_sb", [P, KD, 1])
        idx_sb = sb("idx_sb", [P, B], I32)
        scale_sb = sb("scale_sb", [P, 1])
        shared_gu = sb("shared_gu", [P, 2, KD, IS])
        shared_d = sb("shared_d", [P, SF + 1, D])
        routed_gu = sb("routed_gu", [P, 2, KD, E * I])
        routed_d = sb("routed_d", [P, RC, D])
        ident = sb("ident", [P, P])
        xT_hi = sb("xT_hi", [P, KD, N], F32R)
        xT_lo = sb("xT_lo", [P, KD, N], F32R)
        condT_hi = sb("condT_hi", [P, 8, P], F32R)
        condT_lo = sb("condT_lo", [P, 8, P], F32R)
        xa = sb("xa", [P, HALF])
        xa_hi = sb("xa_hi", [P, HALF], F32R)
        xa_lo = sb("xa_lo", [P, HALF], F32R)
        part_i = sb("part_i", [P, 1], I32)
        part_a = sb("part_a", [P, 1], I32)
        adapter_of_part = sb("adapter_of_part", [P, 1])
        idx_f = sb("idx_f", [P, B])
        adapter_coef = sb("adapter_coef", [P, B])
        hT_hi = sb("hT_hi", [P, KD, N], F32R)
        hT_lo = sb("hT_lo", [P, KD, N], F32R)
        gates_w = sb("gates_w", [P, KD, P])
        gates_hi = sb("gates_hi", [P, KD, P], F32R)
        gates_lo = sb("gates_lo", [P, KD, P], F32R)
        logitsT = sb("logitsT", [E, N])
        sg = sb("sg", [P, N])
        mx = sb("mx", [P, NT])
        shifted = sb("shifted", [P, NT, E])
        expd = sb("expd", [P, NT, E])
        den = sb("den", [P, NT])
        rden = sb("rden", [P, NT])
        probs = sb("probs", [P, NT, E])
        top = sb("top", [P, NT, 8])
        top_i = sb("top_i", [P, NT, 8], U32)
        top_f = sb("top_f", [P, NT, 8])
        experts = sb("experts", [P, E])
        hit = sb("hit", [P, NT, E, TOP_K])
        picked = sb("picked", [P, NT, E])
        topsum = sb("topsum", [P, NT])
        rtop = sb("rtop", [P, NT])
        kept = sb("kept", [P, NT, E])
        comb = sb("comb", [P, NT, E])
        combT = sb("combT", [P, P])
        gu_hi = sb("gu_hi", [P, 2, 2, KD, P], F32R)
        gu_lo = sb("gu_lo", [P, 2, 2, KD, P], F32R)
        dn_hi = sb("dn_hi", [P, 2, D], F32R)
        dn_lo = sb("dn_lo", [P, 2, D], F32R)
        comb_bc = sb("comb_bc", [P, 2, N])
        silu = sb("silu", [P, 2, HALF])
        up = sb("up", [P, 2, HALF])
        inner = sb("inner", [P, 2, HALF])
        inner_hi = sb("inner_hi", [P, 2, HALF], F32R)
        inner_lo = sb("inner_lo", [P, 2, HALF], F32R)
        outT = comb_bc

        acc = [[ctx.enter_context(nc.psum_tensor(f"acc_{o}_{t}", [P, HALF], F32)) for t in range(NH)]
               for o in range(KD)]
        gate_ps = [ctx.enter_context(nc.psum_tensor(f"gate_ps{t}", [P, HALF], F32)) for t in range(NH)]
        up_ps = [ctx.enter_context(nc.psum_tensor(f"up_ps{t}", [P, HALF], F32)) for t in range(NH)]
        wT_ps, abT_ps = gate_ps[0], gate_ps[1]
        routerT_ps = up_ps[0]
        xa_ps = [up_ps[0], up_ps[1]]
        h_ps = acc
        gates_ps = [gate_ps[0], gate_ps[1]]
        tok_ps = up_ps[0]
        combT_ps = gate_ps[0]

        x_in = [sem(f"x_in{t}") for t in range(NH)]
        cond_in = sem("cond_in")
        small_in = sem("small_in")
        shared_in = sem("shared_in")
        routed_in = [sem(f"routed_in{q}") for q in range(LOADS)]
        ident_ready = sem("ident_ready")
        pool_step = sem("pool_step")
        coef_ready = sem("coef_ready")
        condT_ready = sem("condT_ready")
        routerT_ready = sem("routerT_ready")
        xT_ready = sem("xT_ready")
        cond_hi_done = sem("cond_hi_done")
        cond_lo_done = sem("cond_lo_done")
        x_hi_done = sem("x_hi_done")
        x_lo_done = sem("x_lo_done")
        gates_w_done = sem("gates_w_done")
        gates_hi_done = sem("gates_hi_done")
        gates_lo_done = sem("gates_lo_done")
        xa_ready = sem("xa_ready")
        xa_done = sem("xa_done")
        xa_hi_done = sem("xa_hi_done")
        xa_lo_done = sem("xa_lo_done")
        h_ready = sem("h_ready")
        h_hi_done = sem("h_hi_done")
        h_lo_done = sem("h_lo_done")
        gates_ready = sem("gates_ready")
        logits_copied = sem("logits_copied")
        tanh_done = sem("tanh_done")
        sg_done = sem("sg_done")
        tok_ready = sem("tok_ready")
        shifted_done = sem("shifted_done")
        exp_done = sem("exp_done")
        dve_step = sem("dve_step")
        comb_done = sem("comb_done")
        combT_ready = sem("combT_ready")
        combT_copied = sem("combT_copied")
        rows_out = sem("rows_out")
        comb_in = [sem(f"comb_in{b}") for b in range(2)]
        wgu_hi_done = sem("wgu_hi_done")
        wgu_lo_done = sem("wgu_lo_done")
        wdn_hi_done = sem("wdn_hi_done")
        wdn_lo_done = sem("wdn_lo_done")
        gate_ready = sem("gate_ready")
        up_ready = sem("up_ready")
        silu_done = sem("silu_done")
        up_done = sem("up_done")
        inner_done = sem("inner_done")
        inner_hi_done = sem("inner_hi_done")
        inner_lo_done = sem("inner_lo_done")
        down_done = sem("down_done")
        accT_a = sem("accT_a")
        accT_v = sem("accT_v")
        outT_ready = sem("outT_ready")
        out_done = sem("out_done")
        stored = sem("stored")

        def unit_of(f, t):
            return f * NH + t

        def slot_of(f):
            return f % 2

        def shared_parts(f):
            s = slot_of(f)
            if f < SF:
                cols = slice(f * P, (f + 1) * P)
                gu = [(gu_lo[:, s, g, :, :], gu_hi[:, s, g, :, :], shared_gu[:, g, :, cols]) for g in range(2)]
                return gu, [(dn_lo[:, s, :], dn_hi[:, s, :], shared_d[:, f, :])]
            gu = [(gu_lo[:, s, 0, :, g * SR:(g + 1) * SR], gu_hi[:, s, 0, :, g * SR:(g + 1) * SR],
                   shared_gu[:, g, :, SF * P:IS]) for g in range(2)]
            return gu, [(dn_lo[0:SR, s, :], dn_hi[0:SR, s, :], shared_d[0:SR, SF, :])]

        def routed_parts(c, s):
            gu = [(gu_lo[:, s, g, :, :], gu_hi[:, s, g, :, :], routed_gu[:, g, :, bass.ds(c * P, P)])
                  for g in range(2)]
            return gu, [(dn_lo[:, s, :], dn_hi[:, s, :], routed_d[:, bass.ds(c, 1), :].rearrange("p c d -> p (c d)"))]

        block = ctx.enter_context(nc.Block())

        @block.sync
        def _(sp):
            for t in range(NH):
                tiles = slice(t * TPH, (t + 1) * TPH)
                sp.dma_start(x_sb[:, tiles, :], x_tok[:, tiles, :]).then_inc(x_in[t], 16)
            for g, w in enumerate((sh_gate, sh_up)):
                sp.dma_start(shared_gu[:, g, :, :], w.rearrange("(k p) i -> p k i", p=P)).then_inc(shared_in, 16)
            sp.dma_start(shared_d[:, 0:SF, :],
                         sh_down[0:SF * P, :].rearrange("(c p) d -> p c d", p=P)).then_inc(shared_in, 16)
            sp.dma_start(shared_d[0:SR, SF, :], sh_down[SF * P:IS, :]).then_inc(shared_in, 16)
            dn_rows = w_down.rearrange("e i d -> (e i) d").rearrange("(c p) d -> p c d", p=P)
            for q in range(LOADS):
                for g, w in enumerate((w_gate, w_up)):
                    for k in range(KD):
                        dst = routed_gu[:, g, k, q * EL * I:(q + 1) * EL * I].rearrange("p (e i) -> p e i", i=I)
                        src = w[q * EL:(q + 1) * EL, k * P:(k + 1) * P, :].rearrange("e p i -> p e i")
                        sp.dma_start(dst, src).then_inc(routed_in[q], 16)
                cs = slice(q * CL, (q + 1) * CL)
                sp.dma_start(routed_d[:, cs, :], dn_rows[:, cs, :]).then_inc(routed_in[q], 16)
            sp.wait_ge(combT_copied, 1)
            rows = comb_rows.rearrange("(e r) n -> e r n", r=REP)
            for n in range(NT):
                src = combT[n * E:(n + 1) * E, :].unsqueeze(1).to_broadcast([E, REP, P])
                sp.dma_start(rows[:, :, n * P:(n + 1) * P], src).then_inc(rows_out, 16)
            sp.wait_ge(rows_out, 16 * NT)

            def spread(c, pair, b):
                per = P // GRAIN
                src = comb_rows[bass.ds(c * per, per), :].unsqueeze(1).to_broadcast([per, GRAIN, N])
                sp.dma_start(comb_bc[:, b, :], src).then_inc(comb_in[b], 16)

            for b in range(2):
                spread(b, 0, b)
            with sp.Fori(1, RC // 2) as i:
                for b in range(2):
                    sp.wait_ge(up_done, (2 * i + b - 2 + FIRST_ROUTED) * NH + NH)
                    spread(2 * i + b, i, b)
            for t in range(NH):
                tiles = slice(t * TPH, (t + 1) * TPH)
                sp.wait_ge(out_done, 2 * (t + 1))
                sp.dma_start(out_tok[:, tiles, :], x_sb[:, tiles, :]).then_inc(stored, 16)
            sp.wait_ge(stored, 16 * NH)

        @block.gpsimd
        def _(pool):
            nc.gpsimd.memset(ident[:], 0.0).then_inc(pool_step, 1)
            pool.wait_ge(pool_step, 1)
            nc.gpsimd.affine_select(out=ident[:], in_=ident[:], compare_op=ALU.not_equal, fill=1.0, base=0,
                                    pattern=[[-1, P]], channel_multiplier=1).then_inc(ident_ready, 1)
            nc.gpsimd.memset(gates_w[:], 0.0).then_inc(gates_w_done, 1)
            nc.gpsimd.iota(part_i[:], pattern=[[0, 1]], base=0, channel_multiplier=1).then_inc(pool_step, 1)
            nc.gpsimd.iota(experts[:], pattern=[[1, E]], base=0, channel_multiplier=0,
                           allow_small_or_imprecise_dtypes=True).then_inc(pool_step, 1)

            def low_parts(f, s, gu, dn):
                pool.wait_ge(wgu_hi_done, f + 1)
                for dst, hi, raw in gu:
                    last = nc.gpsimd.tensor_tensor(dst, raw, hi.bitcast(F32), ALU.subtract)
                last.then_inc(wgu_lo_done, 1)
                pool.wait_ge(wdn_hi_done, f + 1)
                for dst, hi, raw in dn:
                    last = nc.gpsimd.tensor_tensor(dst, raw, hi.bitcast(F32), ALU.subtract)
                last.then_inc(wdn_lo_done, 1)

            for f in range(FIRST_ROUTED):
                low_parts(f, slot_of(f), *shared_parts(f))
            with pool.Fori(0, RC // 2) as i:
                for b in range(2):
                    low_parts(2 * i + (b + FIRST_ROUTED), b, *routed_parts(2 * i + b, b))

        @block.scalar
        def _(act):
            act.dma_start(cond_w_sb[:], cond_w.rearrange("(k p) d -> p k d", p=P)).then_inc(cond_in, 16)
            act.dma_start(cond_a_sb[:], cond_a.rearrange("a r d -> (a r) d")).then_inc(cond_in, 16)
            for k in range(KD):
                act.dma_start(cond_b_sb[:, k, :, :],
                              cond_b[:, k * P:(k + 1) * P, :].rearrange("a p r -> p a r")).then_inc(cond_in, 16)
            act.dma_start(router_sb[:], router_w).then_inc(cond_in, 16)
            act.dma_start(shw_sb[:], sh_gate_w.rearrange("(k p) o -> p k o", p=P),
                          allow_slow_non_contiguous=True).then_inc(small_in, 16)
            act.dma_start(idx_sb[:], adapter_idx.rearrange("(a b) -> a b", a=1).to_broadcast([P, B])).then_inc(small_in, 16)
            act.dma_start(scale_sb[:], scalings.rearrange("(a o) -> a o", o=1).unsqueeze(1)
                          .to_broadcast([NA, RANK, 1]), allow_slow_non_contiguous=True).then_inc(small_in, 16)

            for j, ps in enumerate((wT_ps, abT_ps)):
                act.wait_ge(condT_ready, j + 1)
                nc.scalar.activation(condT_hi[:, 4 * j:4 * j + 4, :].rearrange("p b c -> p (b c)"), ps[:, :],
                                     ACT.Copy).then_inc(cond_hi_done, 1)
            for t in range(NH):
                for k in range(KD):
                    act.wait_ge(xT_ready, t * KD + k + 1)
                    nc.scalar.activation(xT_hi[:, k, t * HALF:(t + 1) * HALF], acc[k][t][:, :],
                                         ACT.Copy).then_inc(x_hi_done, 1)
            act.wait_ge(gates_w_done, 3)
            nc.scalar.activation(gates_hi[:], gates_w[:], ACT.Copy).then_inc(gates_hi_done, 1)

            def high_parts(gu, dn):
                for _, dst, raw in gu:
                    last = nc.scalar.activation(dst, raw, ACT.Copy)
                last.then_inc(wgu_hi_done, 1)
                for _, dst, raw in dn:
                    last = nc.scalar.activation(dst, raw, ACT.Copy)
                last.then_inc(wdn_hi_done, 1)

            for t in range(NH):
                act.wait_ge(xa_done, t + 1)
                if t:
                    act.wait_ge(h_ready, t * KD)
                nc.scalar.activation(xa_hi[:], xa[:], ACT.Copy).then_inc(xa_hi_done, 1)
                for o in range(KD):
                    act.wait_ge(h_ready, t * KD + o + 1)
                    nc.scalar.activation(hT_hi[:, o, t * HALF:(t + 1) * HALF], h_ps[o][t][:, :],
                                         ACT.Copy).then_inc(h_hi_done, 1)
            act.wait_ge(shared_in, 16 * 4)
            high_parts(*shared_parts(0))
            for t in range(NH):
                cols = slice(t * HALF, (t + 1) * HALF)
                act.wait_ge(gates_ready, t + 1)
                nc.scalar.activation(logitsT[:, cols], gates_ps[t][0:E, :], ACT.Copy).then_inc(logits_copied, 1)
                for q in range(2):
                    last = nc.scalar.activation(sg[q * 64:(q + 1) * 64, cols], gates_ps[t][64:P, :],
                                                ACT.Tanh, scale=0.5)
                last.then_inc(tanh_done, 1)
            act.wait_ge(shifted_done, 1)
            nc.scalar.activation(expd[:], shifted[:], ACT.Exp).then_inc(exp_done, 1)

            def gate_half(f, t, rows=P):
                n = unit_of(f, t)
                act.wait_ge(gate_ready if rows == P else up_ready, n + 1)
                if not (isinstance(n, int) and n < NH):
                    act.wait_ge(inner_done, n - (NH - 1))
                nc.scalar.activation(silu[0:rows, t, :], gate_ps[t][0:rows, :], ACT.Silu).then_inc(silu_done, 1)

            def high_half(f, t, rows=P):
                n = unit_of(f, t)
                act.wait_ge(inner_done, n + 1)
                if not (isinstance(n, int) and n < NH):
                    act.wait_ge(down_done, n - (NH - 1))
                nc.scalar.activation(inner_hi[0:rows, t, :], inner[0:rows, t, :],
                                     ACT.Copy).then_inc(inner_hi_done, 1)

            def chunk(f, parts, rows=P):
                gate_half(f, 0, rows)
                high_half(f, 0, rows)
                if parts:
                    gu, dn = parts
                    first = isinstance(f, int) and f == 0
                    if not first:
                        act.wait_ge(up_ready, unit_of(f, 0))
                    for _, dst, raw in gu:
                        last = nc.scalar.activation(dst, raw, ACT.Copy)
                    last.then_inc(wgu_hi_done, 1)
                gate_half(f, 1, rows)
                if parts:
                    if not first:
                        act.wait_ge(down_done, unit_of(f, 0))
                    for _, dst, raw in dn:
                        last = nc.scalar.activation(dst, raw, ACT.Copy)
                    last.then_inc(wdn_hi_done, 1)
                high_half(f, 1, rows)

            for f in range(FIRST_ROUTED):
                if f + 1 == FIRST_ROUTED:
                    act.wait_ge(routed_in[0], 16 * (2 * KD + 1))
                nxt = shared_parts(f + 1) if f + 1 < FIRST_ROUTED else routed_parts(0, slot_of(f + 1))
                chunk(f, nxt, P if f < SF else SR)

            def pair(i, more=True):
                for b in range(2):
                    chunk(2 * i + (b + FIRST_ROUTED),
                          routed_parts(2 * i + (b + 1), 1 - b) if more or b == 0 else None)

            with act.Fori(0, CL // 2) as i:
                pair(i)
            for q in range(1, LOADS):
                act.wait_ge(routed_in[q], 16 * (2 * KD + 1))
            with act.Fori(CL // 2, RC // 2 - 1) as i:
                pair(i)
            pair(RC // 2 - 1, more=False)
            for t in range(NH):
                act.wait_ge(down_done, unit_of(CHUNKS - 1, t) + 1)
                nc.scalar.activation(outT[:, 0, t * HALF:(t + 1) * HALF], acc[0][t][:, :],
                                     ACT.Copy).then_inc(accT_a, 1)

        @block.vector
        def _(dve):
            steps = [0]

            def step(ins):
                steps[0] += 1
                ins.then_inc(dve_step, 1)
                dve.wait_ge(dve_step, steps[0])

            dve.wait_ge(small_in, 16 * 3)
            dve.wait_ge(pool_step, 3)
            step(nc.vector.tensor_single_scalar(part_a[:], part_i[:], RANK.bit_length() - 1, ALU.arith_shift_right))
            step(nc.vector.tensor_copy(adapter_of_part[:], part_a[:]))
            step(nc.vector.tensor_copy(idx_f[:], idx_sb[:]))
            step(nc.vector.tensor_scalar(adapter_coef[:], idx_f[:], adapter_of_part[:, 0:1], scale_sb[:, 0:1],
                                         ALU.is_equal, ALU.mult))
            for j, ps in enumerate((wT_ps, abT_ps)):
                dve.wait_ge(cond_hi_done, j + 1)
                blocks = slice(4 * j, 4 * j + 4)
                nc.vector.tensor_tensor(condT_lo[:, blocks, :].rearrange("p b c -> p (b c)"), ps[:, :],
                                        condT_hi[:, blocks, :].rearrange("p b c -> p (b c)").bitcast(F32),
                                        ALU.subtract).then_inc(cond_lo_done, 1)
            dve.wait_ge(routerT_ready, 1)
            dve.wait_ge(gates_w_done, 1)
            nc.vector.tensor_copy(gates_w[:, :, 0:E],
                                  routerT_ps[:, 0:KD * E].rearrange("p (k e) -> p k e", e=E)).then_inc(gates_w_done, 1)
            nc.vector.tensor_copy(gates_w[:, :, 64:P], shw_sb[:].to_broadcast([P, KD, 64])).then_inc(gates_w_done, 1)
            for t in range(NH):
                for k in range(KD):
                    cols = slice(t * HALF, (t + 1) * HALF)
                    dve.wait_ge(x_hi_done, t * KD + k + 1)
                    nc.vector.tensor_tensor(xT_lo[:, k, cols], acc[k][t][:, :], xT_hi[:, k, cols].bitcast(F32),
                                            ALU.subtract).then_inc(x_lo_done, 1)
            dve.wait_ge(gates_hi_done, 1)
            nc.vector.tensor_tensor(gates_lo[:], gates_w[:], gates_hi[:].bitcast(F32),
                                    ALU.subtract).then_inc(gates_lo_done, 1)
            for t in range(NH):
                dve.wait_ge(xa_ready, t + 1)
                if t:
                    dve.wait_ge(xa_lo_done, t)
                    dve.wait_ge(xa_hi_done, t)
                nc.vector.tensor_tensor(
                    xa[:].rearrange("p (b t) -> p b t", t=T), xa_ps[t][:, :].rearrange("p (b t) -> p b t", t=T),
                    adapter_coef[:, t * BH:(t + 1) * BH].unsqueeze(2).to_broadcast([P, BH, T]),
                    ALU.mult).then_inc(xa_done, 1)
                dve.wait_ge(xa_hi_done, t + 1)
                nc.vector.tensor_tensor(xa_lo[:], xa[:], xa_hi[:].bitcast(F32), ALU.subtract).then_inc(xa_lo_done, 1)
                for o in range(KD):
                    cols = slice(t * HALF, (t + 1) * HALF)
                    dve.wait_ge(h_hi_done, t * KD + o + 1)
                    nc.vector.tensor_tensor(hT_lo[:, o, cols], h_ps[o][t][:, :], hT_hi[:, o, cols].bitcast(F32),
                                            ALU.subtract).then_inc(h_lo_done, 1)
            def over_experts(v):
                return v[:].unsqueeze(2).to_broadcast([P, NT, E])

            tok = tok_ps[:, 0:NT * E].rearrange("p (n e) -> p n e", e=E)
            dve.wait_ge(tok_ready, 1)
            step(nc.vector.tensor_reduce(mx[:], tok, AX_X, ALU.max))
            nc.vector.tensor_tensor(shifted[:], tok, over_experts(mx), ALU.subtract).then_inc(shifted_done, 1)
            dve.wait_ge(tanh_done, NH)
            nc.vector.tensor_scalar(sg[:], sg[:], 0.5, 0.5, ALU.mult, ALU.add).then_inc(sg_done, 1)
            dve.wait_ge(exp_done, 1)
            step(nc.vector.tensor_reduce(den[:], expd[:], AX_X, ALU.add))
            step(nc.vector.reciprocal(rden[:], den[:]))
            step(nc.vector.tensor_tensor(probs[:], expd[:], over_experts(rden), ALU.mult))
            dve.wait_ge(sg_done, 1)

            def unit(f, t, weight, rows=P, up_rows=None):
                n = unit_of(f, t)
                static = isinstance(n, int)
                up_src = up_ps[t][0:rows, :] if up_rows is None else gate_ps[t][up_rows, :]
                dve.wait_ge(up_ready, n + 1)
                if not (static and n < NH):
                    dve.wait_ge(inner_done, n - (NH - 1))
                nc.vector.tensor_tensor(up[0:rows, t, :], up_src, weight, ALU.mult).then_inc(up_done, 1)
                dve.wait_ge(up_done, n + 1)
                dve.wait_ge(silu_done, n + 1)
                if not (static and n < NH):
                    dve.wait_ge(inner_hi_done, n - (NH - 1))
                    dve.wait_ge(inner_lo_done, n - (NH - 1))
                nc.vector.tensor_tensor(inner[0:rows, t, :], up[0:rows, t, :], silu[0:rows, t, :],
                                        ALU.mult).then_inc(inner_done, 1)
                dve.wait_ge(inner_hi_done, n + 1)
                nc.vector.tensor_tensor(inner_lo[0:rows, t, :], inner[0:rows, t, :],
                                        inner_hi[0:rows, t, :].bitcast(F32),
                                        ALU.subtract).then_inc(inner_lo_done, 1)

            def choose():
                for n in range(NT):
                    last = nc.vector.max(top[:, n, :], probs[:, n, :])
                step(last)
                for n in range(NT):
                    last = nc.vector.max_index(top_i[:, n, :], top[:, n, :], probs[:, n, :])
                step(last)

            def weigh():
                step(nc.vector.tensor_copy(top_f[:], top_i[:]))
                step(nc.vector.tensor_tensor(
                    hit[:], experts[:].unsqueeze(1).unsqueeze(3).to_broadcast([P, NT, E, TOP_K]),
                    top_f[:, :, 0:TOP_K].unsqueeze(2).to_broadcast([P, NT, E, TOP_K]), ALU.is_equal))
                step(nc.vector.tensor_reduce(picked[:], hit[:], AX_X, ALU.add))
                step(nc.vector.tensor_reduce(topsum[:], top[:, :, 0:TOP_K], AX_X, ALU.add))
                step(nc.vector.tensor_scalar(topsum[:], topsum[:], 1e-9, None, ALU.max))
                step(nc.vector.reciprocal(rtop[:], topsum[:]))
                step(nc.vector.tensor_tensor(kept[:], picked[:], probs[:], ALU.mult))
                nc.vector.tensor_tensor(comb[:], kept[:], over_experts(rtop), ALU.mult).then_inc(comb_done, 1)

            for f in range(FIRST_ROUTED):
                for t in range(NH):
                    cols = slice(t * HALF, (t + 1) * HALF)
                    if f < SF:
                        unit(f, t, sg[:, cols])
                    else:
                        unit(f, t, sg[0:SR, cols], SR, slice(SR, 2 * SR))
                    if (f, t) == (0, 0):
                        choose()
                    if (f, t) == (0, 1):
                        weigh()
                    if (f, t) == (1, 1):
                        dve.wait_ge(combT_ready, 1)
                        nc.vector.tensor_copy(combT[:], combT_ps[:, 0:P]).then_inc(combT_copied, 1)

            def pair(i):
                for b in range(2):
                    dve.wait_ge(comb_in[b], (i + 1) * 16)
                    for t in range(NH):
                        unit(2 * i + (b + FIRST_ROUTED), t, comb_bc[:, b, t * HALF:(t + 1) * HALF])

            with dve.Fori(0, RC // 2) as i:
                pair(i)
            for t in range(NH):
                dve.wait_ge(down_done, unit_of(CHUNKS - 1, t) + 1)
                nc.vector.tensor_copy(outT[:, 1, t * HALF:(t + 1) * HALF], acc[1][t][:, :]).then_inc(accT_v, 1)
            for t in range(NH):
                for q, ps in enumerate((gate_ps[t], up_ps[t])):
                    tiles = slice(t * TPH + 2 * q, t * TPH + 2 * q + 2)
                    dve.wait_ge(outT_ready, 2 * t + q + 1)
                    nc.vector.tensor_tensor(x_sb[:, tiles, :].rearrange("p n d -> p (n d)"), ps[:, :],
                                            x_sb[:, tiles, :].rearrange("p n d -> p (n d)"),
                                            ALU.add).then_inc(out_done, 1)

        @block.tensor
        def _(pe):
            def product(dst, pairs, first=True, last=True, begun=None):
                terms = []
                for w_hi, w_lo, m_hi, m_lo in pairs:
                    terms += [(w_hi, m_hi), (w_hi, m_lo), (w_lo, m_hi)]
                for j, (w, m) in enumerate(terms):
                    mm = nc.tensor.matmul(dst, w, m, start=first and j == 0, stop=last and j == len(terms) - 1)
                    if j == 0 and begun is not None:
                        mm.then_inc(begun, 1)
                return mm

            pe.wait_ge(ident_ready, 1)
            pe.wait_ge(cond_in, 16 * (3 + KD))
            for k in range(KD):
                for o in range(KD):
                    mm = nc.tensor.transpose(wT_ps[:, (KD * k + o) * P:(KD * k + o + 1) * P],
                                             cond_w_sb[:, o, k * P:(k + 1) * P], ident[:])
            mm.then_inc(condT_ready, 1)
            for k in range(KD):
                nc.tensor.transpose(abT_ps[:, k * P:(k + 1) * P], cond_a_sb[:, k * P:(k + 1) * P], ident[:])
            for o in range(KD):
                mm = nc.tensor.transpose(abT_ps[:, (KD + o) * P:(KD + o + 1) * P],
                                         cond_b_sb[:, o, :, :].rearrange("p a r -> p (a r)"), ident[:])
            mm.then_inc(condT_ready, 1)
            for k in range(KD):
                mm = nc.tensor.transpose(routerT_ps[:, k * E:(k + 1) * E], router_sb[:, k * P:(k + 1) * P],
                                         ident[0:E, 0:E])
            mm.then_inc(routerT_ready, 1)
            for t in range(NH):
                pe.wait_ge(x_in[t], 16)
                for k in range(KD):
                    for j in range(TPH):
                        mm = nc.tensor.transpose(acc[k][t][:, j * P:(j + 1) * P],
                                                 x_sb[:, t * TPH + j, k * P:(k + 1) * P], ident[:])
                    mm.then_inc(xT_ready, 1)

            def w_block(k, o):
                return condT_hi[:, KD * k + o, :], condT_lo[:, KD * k + o, :]

            def a_block(k):
                return condT_hi[:, 4 + k, :], condT_lo[:, 4 + k, :]

            def b_block(o):
                return condT_hi[:, 4 + KD + o, :], condT_lo[:, 4 + KD + o, :]

            pe.wait_ge(cond_lo_done, 2)
            pe.wait_ge(gates_w_done, 3)
            for t in range(NH):
                cols = slice(t * HALF, (t + 1) * HALF)
                pe.wait_ge(x_lo_done, (t + 1) * KD)
                product(xa_ps[t][:, :], [(*a_block(k), xT_hi[:, k, cols], xT_lo[:, k, cols])
                                         for k in range(KD)]).then_inc(xa_ready, 1)
                for o in range(KD):
                    product(h_ps[o][t][:, :], [(*w_block(k, o), xT_hi[:, k, cols], xT_lo[:, k, cols])
                                               for k in range(KD)], last=False)
                pe.wait_ge(xa_lo_done, t + 1)
                for o in range(KD):
                    mm = product(h_ps[o][t][:, :], [(*b_block(o), xa_hi[:], xa_lo[:])], first=False)
                    mm.then_inc(h_ready, 1)
            pe.wait_ge(gates_lo_done, 1)
            for t in range(NH):
                cols = slice(t * HALF, (t + 1) * HALF)
                pe.wait_ge(h_lo_done, (t + 1) * KD)
                product(gates_ps[t][:, :], [(gates_hi[:, k, :], gates_lo[:, k, :], hT_hi[:, k, cols], hT_lo[:, k, cols])
                                            for k in range(KD)]).then_inc(gates_ready, 1)
            pe.wait_ge(logits_copied, NH)
            pe.wait_ge(xa_done, NH)
            for n in range(NT):
                mm = nc.tensor.transpose(tok_ps[:, n * E:(n + 1) * E], logitsT[:, n * P:(n + 1) * P],
                                         ident[0:E, 0:E])
            mm.then_inc(tok_ready, 1)
            pe.wait_ge(tanh_done, NH)

            def gate_up(f, t, s, short=False, after_short=False):
                n = unit_of(f, t)
                fresh = isinstance(n, int) and n < NH
                cols = slice(t * HALF, (t + 1) * HALF)
                if t == 0:
                    pe.wait_ge(wgu_lo_done, f + 1)
                def operands(g):
                    return [(gu_hi[:, s, g, k, :], gu_lo[:, s, g, k, :], hT_hi[:, k, cols], hT_lo[:, k, cols])
                            for k in range(KD)]
                if not fresh:
                    pe.wait_ge(silu_done, n - (NH - 1))
                if after_short:
                    pe.wait_ge(up_done, n - (NH - 1))
                if short:
                    product(gate_ps[t][:, :], operands(0), begun=gate_ready).then_inc(up_ready, 1)
                    return
                product(gate_ps[t][:, :], operands(0)).then_inc(gate_ready, 1)
                if fresh:
                    pe.wait_ge(shifted_done, 1)
                else:
                    pe.wait_ge(up_done, n - (NH - 1))
                product(up_ps[t][:, :], operands(1)).then_inc(up_ready, 1)

            def down(f, t, s, first=False, last=False, rows=P):
                n = unit_of(f, t)
                if t == 0:
                    pe.wait_ge(wdn_lo_done, f + 1)
                pe.wait_ge(inner_lo_done, n + 1)
                for o in range(KD):
                    w = slice(o * P, (o + 1) * P)
                    mm = product(acc[o][t][:, :], [(dn_hi[0:rows, s, w], dn_lo[0:rows, s, w],
                                                    inner_hi[0:rows, t, :], inner_lo[0:rows, t, :])],
                                 first=first, last=last)
                mm.then_inc(down_done, 1)

            for f in range(FIRST_ROUTED):
                short = f == SF
                if f == 2:
                    pe.wait_ge(comb_done, 1)
                    pe.wait_ge(silu_done, unit_of(f, 0) - (NH - 1))
                    nc.tensor.transpose(combT_ps[:, 0:P], comb[:].rearrange("p n e -> p (n e)"),
                                        ident[:]).then_inc(combT_ready, 1)
                    pe.wait_ge(combT_copied, 1)
                for t in range(NH):
                    gate_up(f, t, slot_of(f), short)
                    if t:
                        down(f, 0, slot_of(f), first=f == 0, rows=SR if short else P)
                    elif f:
                        down(f - 1, 1, slot_of(f - 1), first=f == 1)

            def pair(i, after_short=False, last=False):
                for b in range(2):
                    f = 2 * i + (b + FIRST_ROUTED)
                    gate_up(f, 0, b, after_short=after_short and b == 0)
                    down(f - 1, 1, 1 - b, rows=SR if after_short and b == 0 else P)
                    gate_up(f, 1, b, after_short=after_short and b == 0)
                    down(f, 0, b, last=last and b == 1)

            pair(0, after_short=True)
            with pe.Fori(1, RC // 2 - 1) as i:
                pair(i)
            pair(RC // 2 - 1, last=True)
            down(CHUNKS - 1, 1, 1, last=True)
            for t in range(NH):
                pe.wait_ge(accT_a, t + 1)
                pe.wait_ge(accT_v, t + 1)
                pe.wait_ge(up_done, unit_of(CHUNKS - 1, t) + 1)
                pe.wait_ge(silu_done, unit_of(CHUNKS - 1, t) + 1)
                for q, ps in enumerate((gate_ps[t], up_ps[t])):
                    for j in range(2):
                        n = t * TPH + 2 * q + j
                        for k in range(KD):
                            mm = nc.tensor.transpose(ps[:, (j * KD + k) * P:(j * KD + k + 1) * P],
                                                     outT[:, k, n * P:(n + 1) * P], ident[:])
                    mm.then_inc(outT_ready, 1)


_INS = ['x', 'itok_B_0_6', 'L0_cond_W', 'L0_cond_A', 'L0_cond_Bm', 'L0_cond_scalings', 'L0_ffn_router_w',
        'L0_ffn_w_gate', 'L0_ffn_w_up', 'L0_ffn_w_down', 'L0_ffn_sh_gate', 'L0_ffn_sh_up', 'L0_ffn_sh_down',
        'L0_ffn_sh_gate_w']


def kernel(**inputs):
    import numpy as _np
    import concourse.bacc as _bacc
    from concourse import mybir as _mybir
    from concourse.bass_utils import run_bass_kernel_spmd as _run

    nc = _bacc.Bacc("TRN2", target_bir_lowering=False, num_devices=1)
    arrays, args = {}, []
    for name in _INS:
        a = _np.ascontiguousarray(inputs[name])
        arrays[f"in_{name}_dram"] = a
        args.append(nc.dram_tensor(f"in_{name}_dram", a.shape, _mybir.dt.from_np(a.dtype), kind="ExternalInput").ap())
    out = nc.dram_tensor("out_0_dram", inputs["x"].shape, _mybir.dt.float32, kind="ExternalOutput").ap()
    adaln_moe_ffn(nc, *args, out)
    r = _run(nc, [arrays], core_ids=[0])
    return r.results[0]["out_0_dram"]
```

```python
from contextlib import ExitStack

import concourse.bass as bass
from concourse import mybir

F32 = mybir.dt.float32
F32R = mybir.dt.float32r
I32 = mybir.dt.int32
U32 = mybir.dt.uint32
BF16 = mybir.dt.bfloat16
FP16 = mybir.dt.float16
ALU = mybir.AluOpType
ACT = mybir.ActivationFunctionType
AX_X = mybir.AxisListType.X

P = 128
HALF = 512
TOP_K = 4


def adaln_moe_ffn(nc, x, adapter_idx, cond_w, cond_a, cond_b, scalings, router_w, w_gate, w_up,
                  w_down, sh_gate, sh_up, sh_down, sh_gate_w, out):
    B, T, D = x.shape
    N = B * T
    NT = N // P
    KD = D // P
    NH = N // HALF
    TPH = HALF // P
    NA, RANK, _ = cond_a.shape
    E, _, I = w_gate.shape
    IS = sh_gate.shape[1]
    SF = IS // P
    SR = IS - SF * P
    SHARED = SF + 1
    TILES = (N * TOP_K - E) // P + E
    PAD = P
    ROW = D + E
    IR = I - P
    RING = 4
    LAPS = (TILES - 4 - 3) // RING
    WARM = 8
    LG = 32
    LOADS = 2
    EL = E // LOADS
    assert NA * RANK == P and 2 * SR == P and NH == 2 and KD == 2 and NT == 8 and 0 < IR <= P
    assert N * TOP_K <= TILES * P and P == 1 << 7 and TILES == RING * LAPS + 7
    BH = B // NH

    x_tok = x.rearrange("b t d -> (b t) d").rearrange("(n p) d -> p n d", p=P)
    out_tok = out.rearrange("b t d -> (b t) d").rearrange("(n p) d -> p n d", p=P)
    h_rows = nc.dram_tensor("h_rows", [N + PAD, ROW], F32, kind="Internal").ap()
    sums = [nc.dram_tensor(f"sums{b}", [N + PAD, D], F32, kind="Internal").ap() for b in range(2)]

    with ExitStack() as ctx:
        def sb(name, shape, dt=F32):
            return ctx.enter_context(nc.sbuf_tensor(name, shape, dt))

        def sem(name):
            return ctx.enter_context(nc.semaphore(name))

        x_sb = sb("x_sb", [P, NT, D])
        router_sb = sb("router_sb", [E, D])
        shw_sb = sb("shw_sb", [P, KD, 1])
        idx_sb = sb("idx_sb", [P, B], I32)
        scale_sb = sb("scale_sb", [P, 1])
        shared_gu = sb("shared_gu", [P, 2, KD, IS])
        shared_d = sb("shared_d", [P, SF + 1, D])
        routed_gu = sb("routed_gu", [P, KD, E, 2 * I])
        routed_d = sb("routed_d", [P, E, 2, D])
        ident = sb("ident", [P, P])
        part_i = sb("part_i", [P, 1], I32)
        part_a = sb("part_a", [P, 1], I32)
        adapter_of_part = sb("adapter_of_part", [P, 1])
        idx_f = sb("idx_f", [P, B])
        adapter_coef = sb("adapter_coef", [P, B])
        hT_hi = sb("hT_hi", [P, KD, N], F32R)
        hT_lo = sb("hT_lo", [P, KD, N], F32R)
        gates_w = sb("gates_w", [P, KD, LG])
        gates_hi = sb("gates_hi", [P, KD, LG], F32R)
        gates_lo = sb("gates_lo", [P, KD, LG], F32R)
        hT = sb("hT", [P, KD, N])
        sg = sb("sg", [P, NT])
        mx = sb("mx", [P, NT])
        shifted = sb("shifted", [P, NT, E])
        expd = sb("expd", [P, NT, E])
        den = sb("den", [P, NT])
        rden = sb("rden", [P, NT])
        probs = sb("probs", [P, NT, E])
        top = sb("top", [P, NT, 8])
        top_i = sb("top_i", [P, NT, 8], U32)
        top_f = sb("top_f", [P, NT, 8])
        experts = sb("experts", [P, E])
        hit = sb("hit", [P, NT, TOP_K, E])
        picked = sb("picked", [P, NT, E])
        topsum = sb("topsum", [P, NT])
        rtop = sb("rtop", [P, NT])
        kept = sb("kept", [P, NT, E])
        h_row = sb("h_row", [P, NT, ROW])
        zeros = sb("zeros", [P, ROW])
        before = sb("before", [P, P], BF16)
        ones = sb("ones", [P, P], BF16)
        picked_b = sb("picked_b", [P, NT, E], BF16)
        below = sb("below", [P, E, E])
        counts = sb("counts", [P, NT * E + E])
        tiles_i = sb("tiles_i", [P, E], I32)
        tiles_s = sb("tiles_s", [P, E], I32)
        tiles_f = sb("tiles_f", [P, E])
        tiles_b = sb("tiles_b", [P, E, E])
        begin = sb("begin", [P, E])
        end = sb("end", [P, E])
        slot_e = sb("slot_e", [P, NT, E])
        slot_k = sb("slot_k", [P, NT, TOP_K])
        slot_i = sb("slot_i", [P, NT, TOP_K], I32)
        lane_i = sb("lane_i", [P, NT, TOP_K], I32)
        tile_i = sb("tile_i", [P, NT, TOP_K], I32)
        lane_f = sb("lane_f", [P, NT, TOP_K])
        tile_f = sb("tile_f", [P, NT, TOP_K])
        lanes = sb("lanes", [P, P], BF16)
        tiles = sb("tiles", [P, TILES])
        token1 = sb("token1", [P, NT])
        empty1 = sb("empty1", [P, 1])
        expert_f = sb("expert_f", [1, TILES])
        expert_of = sb("expert_of", [1, TILES], I32)
        gu_hi = sb("gu_hi", [P, 2, 2, KD, P], F32R)
        gu_lo = sb("gu_lo", [P, 2, 2, KD, P], F32R)
        dn_hi = sb("dn_hi", [P, 2, D], F32R)
        dn_lo = sb("dn_lo", [P, 2, D], F32R)
        outer, ctx = ctx, ExitStack()
        cond_w_sb = sb("cond_w_sb", [P, KD, D])
        cond_a_sb = sb("cond_a_sb", [P, D])
        cond_b_sb = sb("cond_b_sb", [P, KD, NA, RANK])
        xT_hi = sb("xT_hi", [P, KD, N], F32R)
        xT_lo = sb("xT_lo", [P, KD, N], F32R)
        condT_hi = sb("condT_hi", [P, 8, P], F32R)
        condT_lo = sb("condT_lo", [P, 8, P], F32R)
        xa = sb("xa", [P, HALF])
        xa_hi = sb("xa_hi", [P, HALF], F32R)
        xa_lo = sb("xa_lo", [P, HALF], F32R)
        logitsT = sb("logitsT", [LG, N])
        ctx.close()
        ctx = outer
        lane_hot = sb("lane_hot", [P, NT, TOP_K, P], BF16)
        tile_hot = sb("tile_hot", [P, NT, TOP_K, TILES], FP16)
        vacant = sb("vacant", [P, TILES])
        slot_token = sb("slot_token", [P, TILES], U32)
        begun = sb("begun", [P, TILES, E], BF16)
        ended = sb("ended", [P, TILES, E], BF16)
        gather_id = sb("gather_id", [P, RING], U32)
        add_id = sb("add_id", [P, RING], U32)
        rows = sb("rows", [P, RING, ROW])
        w_e = sb("w_e", [P, 2, E])
        w_slot = sb("w_slot", [P, RING])
        silu = sb("silu", [P, 2, HALF])
        inner = sb("inner", [P, 2, HALF])
        inner_hi = sb("inner_hi", [P, 2, HALF], F32R)
        inner_lo = sb("inner_lo", [P, 2, HALF], F32R)
        hgT = sb("hgT", [P, 2, KD, P])
        r_silu = sb("r_silu", [P, 2, I])
        r_inner = sb("r_inner", [P, 2, I])
        innerT = sb("innerT", [P, 2, 2, P])
        y = sb("y", [P, RING, D])
        sharedT = hT
        sum_sb = [hT[:].rearrange("p k n -> p (k n)").rearrange("p (n d) -> p n d", d=D), h_row[:, :, 0:D]]

        acc = [[ctx.enter_context(nc.psum_tensor(f"acc_{o}_{t}", [P, HALF], F32)) for t in range(NH)]
               for o in range(KD)]
        gate_ps = [ctx.enter_context(nc.psum_tensor(f"gate_ps{t}", [P, HALF], F32)) for t in range(NH)]
        up_ps = [ctx.enter_context(nc.psum_tensor(f"up_ps{t}", [P, HALF], F32)) for t in range(NH)]
        wT_ps, abT_ps = gate_ps[0], gate_ps[1]
        routerT_ps = up_ps[0]
        xa_ps = [up_ps[0], up_ps[1]]
        h_ps = acc
        gates_ps = [acc[0][0], acc[0][1]]
        tok_ps = acc[1][0]
        hrow_ps = [acc[0][0], acc[0][1], acc[1][1], acc[1][0]]
        count_ps = gate_ps[0]
        token_ps = gate_ps[1]
        rgu_ps = gate_ps
        hg_ps = up_ps
        innerT_ps = acc[0]
        y_ps = acc[1]

        x_in = [sem(f"x_in{t}") for t in range(NH)]
        cond_in = sem("cond_in")
        small_in = sem("small_in")
        shared_in = sem("shared_in")
        routed_in = [sem(f"routed_in{q}") for q in range(LOADS)]
        ident_ready = sem("ident_ready")
        pool_step = sem("pool_step")
        coef_ready = sem("coef_ready")
        condT_ready = sem("condT_ready")
        routerT_ready = sem("routerT_ready")
        xT_ready = sem("xT_ready")
        cond_hi_done = sem("cond_hi_done")
        cond_lo_done = sem("cond_lo_done")
        x_hi_done = sem("x_hi_done")
        x_lo_done = sem("x_lo_done")
        gates_w_done = sem("gates_w_done")
        gates_hi_done = sem("gates_hi_done")
        gates_lo_done = sem("gates_lo_done")
        xa_ready = sem("xa_ready")
        xa_done = sem("xa_done")
        xa_hi_done = sem("xa_hi_done")
        xa_lo_done = sem("xa_lo_done")
        h_ready = sem("h_ready")
        h_hi_done = sem("h_hi_done")
        h_lo_done = sem("h_lo_done")
        gates_ready = sem("gates_ready")
        logits_copied = sem("logits_copied")
        tanh_done = sem("tanh_done")
        sg_done = sem("sg_done")
        tok_ready = sem("tok_ready")
        shifted_done = sem("shifted_done")
        exp_done = sem("exp_done")
        dve_step = sem("dve_step")
        hT_done = sem("hT_done")
        hrow_ready = sem("hrow_ready")
        hrow_copied = sem("hrow_copied")
        zeros_done = sem("zeros_done")
        picked_done = sem("picked_done")
        count_ready = sem("count_ready")
        count_copied = sem("count_copied")
        tile_f_done = sem("tile_f_done")
        ended_done = sem("ended_done")
        hot_done = sem("hot_done")
        tile_hot_done = sem("tile_hot_done")
        token_ready = sem("token_ready")
        token_done = sem("token_done")
        expert_done = sem("expert_done")
        rows_out = sem("rows_out")
        sums_zero = sem("sums_zero")
        rows_in = [sem(f"rows_in{b}") for b in range(RING)]
        added = [sem(f"added{b}") for b in range(2)]
        pool_clear = sem("pool_clear")
        gather_id_done = sem("gather_id_done")
        add_id_done = sem("add_id_done")
        w_part = sem("w_part")
        w_done = sem("w_done")
        hg_ready = sem("hg_ready")
        hg_copied = sem("hg_copied")
        rgu_ready = sem("rgu_ready")
        r_silu_done = sem("r_silu_done")
        r_inner_done = sem("r_inner_done")
        innerT_ready = sem("innerT_ready")
        innerT_copied = sem("innerT_copied")
        y_ready = sem("y_ready")
        y_copied = sem("y_copied")
        sum_in = [[sem(f"sum_in{b}_{q}") for q in range(NT // 2)] for b in range(2)]
        base_done = sem("base_done")
        sum_done = sem("sum_done")
        comb_done = sem("comb_done")
        wgu_hi_done = sem("wgu_hi_done")
        wgu_lo_done = sem("wgu_lo_done")
        wdn_hi_done = sem("wdn_hi_done")
        wdn_lo_done = sem("wdn_lo_done")
        gate_ready = sem("gate_ready")
        up_ready = sem("up_ready")
        silu_done = sem("silu_done")
        inner_done = sem("inner_done")
        inner_hi_done = sem("inner_hi_done")
        inner_lo_done = sem("inner_lo_done")
        down_done = sem("down_done")
        accT_a = sem("accT_a")
        accT_v = sem("accT_v")
        outT_ready = sem("outT_ready")
        out_done = sem("out_done")
        stored = sem("stored")

        def unit_of(f, t):
            return f * NH + t

        def slot_of(f):
            return f % 2

        def shared_parts(f):
            s = slot_of(f)
            if f < SF:
                cols = slice(f * P, (f + 1) * P)
                gu = [(gu_lo[:, s, g, :, :], gu_hi[:, s, g, :, :], shared_gu[:, g, :, cols]) for g in range(2)]
                return gu, [(dn_lo[:, s, :], dn_hi[:, s, :], shared_d[:, f, :])]
            gu = [(gu_lo[:, s, 0, :, g * SR:(g + 1) * SR], gu_hi[:, s, 0, :, g * SR:(g + 1) * SR],
                   shared_gu[:, g, :, SF * P:IS]) for g in range(2)]
            return gu, [(dn_lo[0:SR, s, :], dn_hi[0:SR, s, :], shared_d[0:SR, SF, :])]

        def tile(j, c):
            return RING * j + c

        def lap(j, c):
            return j + c // RING

        def turn(j, c):
            return (RING // 2) * j + c // 2

        def has(i, before):
            return not isinstance(i, int) or i >= before

        block = ctx.enter_context(nc.Block())

        @block.sync
        def _(sp):
            for t in range(NH):
                tiles = slice(t * TPH, (t + 1) * TPH)
                sp.dma_start(x_sb[:, tiles, :], x_tok[:, tiles, :]).then_inc(x_in[t], 16)
                if t == 0:
                    sp.dma_start(cond_a_sb[:], cond_a.rearrange("a r d -> (a r) d")).then_inc(cond_in, 16)
            sp.dma_start(router_sb[:], router_w).then_inc(cond_in, 16)
            for g, w in enumerate((sh_gate, sh_up)):
                sp.dma_start(shared_gu[:, g, :, :], w.rearrange("(k p) i -> p k i", p=P)).then_inc(shared_in, 16)
            sp.dma_start(shared_d[:, 0:SF, :],
                         sh_down[0:SF * P, :].rearrange("(c p) d -> p c d", p=P)).then_inc(shared_in, 16)
            sp.dma_start(shared_d[0:SR, SF, :], sh_down[SF * P:IS, :]).then_inc(shared_in, 16)
            for q in range(LOADS):
                es = slice(q * EL, (q + 1) * EL)
                for g, w in enumerate((w_gate, w_up)):
                    for k in range(KD):
                        sp.dma_start(routed_gu[:, k, es, g * I:(g + 1) * I],
                                     w[es, k * P:(k + 1) * P, :].rearrange("e p i -> p e i")).then_inc(routed_in[q], 16)
                sp.dma_start(routed_d[:, es, 0, :],
                             w_down[es, 0:P, :].rearrange("e p d -> p e d")).then_inc(routed_in[q], 16)
                sp.dma_start(routed_d[0:IR, es, 1, :],
                             w_down[es, P:I, :].rearrange("e p d -> p e d")).then_inc(routed_in[q], 16)
            sp.wait_ge(zeros_done, 1)
            sp.dma_start(h_rows[N:N + PAD, :], zeros[:]).then_inc(rows_out, 16)
            for b in range(2):
                sp.dma_start(sums[b].rearrange("(n p) d -> p n d", p=P),
                             zeros[:, 0:D].unsqueeze(1).to_broadcast([P, NT + PAD // P, D])).then_inc(sums_zero, 16)
            sp.wait_ge(comb_done, 1)
            sp.wait_ge(hrow_copied, NT // 2)
            sp.dma_start(h_rows[0:N, :].rearrange("(n p) c -> p n c", p=P), h_row[:]).then_inc(rows_out, 16)
            for b in (1, 0):
                sp.wait_ge(added[b], 16 * ((TILES - b + 1) // 2))
                for q in range(NT // 2):
                    tk = slice(2 * q, 2 * q + 2)
                    sp.dma_start(sum_sb[b][:, tk, :],
                                 sums[b][0:N, :].rearrange("(n p) d -> p n d", p=P)[:, tk, :]).then_inc(sum_in[b][q], 16)
            for q in range(NT // 2):
                tk = slice(2 * q, 2 * q + 2)
                sp.wait_ge(out_done, q + 1)
                sp.dma_start(out_tok[:, tk, :], sum_sb[0][:, tk, :]).then_inc(stored, 16)
            sp.wait_ge(stored, 16 * (NT // 2))

        @block.gpsimd
        def _(pool):
            nc.gpsimd.memset(ident[:], 0.0).then_inc(pool_step, 1)
            pool.wait_ge(pool_step, 1)
            nc.gpsimd.affine_select(out=ident[:], in_=ident[:], compare_op=ALU.not_equal, fill=1.0, base=0,
                                    pattern=[[-1, P]], channel_multiplier=1).then_inc(ident_ready, 1)
            nc.gpsimd.memset(gates_w[:], 0.0).then_inc(gates_w_done, 1)
            nc.gpsimd.iota(part_i[:], pattern=[[0, 1]], base=0, channel_multiplier=1).then_inc(pool_step, 1)
            nc.gpsimd.iota(experts[:], pattern=[[1, E]], base=0, channel_multiplier=0,
                           allow_small_or_imprecise_dtypes=True).then_inc(pool_step, 1)
            nc.gpsimd.memset(zeros[:], 0.0).then_inc(zeros_done, 1)
            nc.gpsimd.memset(before[:], 1.0).then_inc(pool_step, 1)
            nc.gpsimd.memset(ones[:], 1.0).then_inc(pool_step, 1)
            nc.gpsimd.memset(below[:], 1.0).then_inc(pool_step, 1)
            pool.wait_ge(pool_step, 6)
            nc.gpsimd.affine_select(out=before[:], in_=before[:], compare_op=ALU.is_gt, fill=0.0, base=0,
                                    pattern=[[1, P]], channel_multiplier=-1).then_inc(pool_step, 1)
            nc.gpsimd.affine_select(out=below[:], in_=below[:], compare_op=ALU.is_gt, fill=0.0, base=0,
                                    pattern=[[1, E], [-1, E]], channel_multiplier=0).then_inc(pool_step, 1)
            nc.gpsimd.iota(lanes[:], pattern=[[1, P]], base=0, channel_multiplier=0,
                           allow_small_or_imprecise_dtypes=True).then_inc(pool_step, 1)
            nc.gpsimd.iota(tiles[:], pattern=[[1, TILES]], base=0, channel_multiplier=0,
                           allow_small_or_imprecise_dtypes=True).then_inc(pool_step, 1)
            nc.gpsimd.iota(token1[:], pattern=[[P, NT]], base=1, channel_multiplier=1,
                           allow_small_or_imprecise_dtypes=True).then_inc(pool_step, 1)
            nc.gpsimd.iota(empty1[:], pattern=[[0, 1]], base=N + 1, channel_multiplier=1,
                           allow_small_or_imprecise_dtypes=True).then_inc(pool_step, 1)

            def low_parts(f, s, gu, dn):
                pool.wait_ge(wgu_hi_done, f + 1)
                for dst, hi, raw in gu:
                    last = nc.gpsimd.tensor_tensor(dst, raw, hi.bitcast(F32), ALU.subtract)
                last.then_inc(wgu_lo_done, 1)
                pool.wait_ge(wdn_hi_done, f + 1)
                for dst, hi, raw in dn:
                    last = nc.gpsimd.tensor_tensor(dst, raw, hi.bitcast(F32), ALU.subtract)
                last.then_inc(wdn_lo_done, 1)

            def tile_hots(tiles_of):
                pool.wait_ge(tile_f_done, 1)
                for n in tiles_of:
                    for k in range(TOP_K):
                        last = nc.gpsimd.tensor_scalar(tile_hot[:, n, k, :], tiles[:], tile_f[:, n, k:k + 1],
                                                       token1[:, n:n + 1], ALU.is_equal, ALU.mult)
                    last.then_inc(tile_hot_done, 1)

            hots_at = {3: (0,), 4: (2, 4), 5: (6,)}
            for f in range(SHARED):
                if f in hots_at:
                    tile_hots(hots_at[f])
                low_parts(f, slot_of(f), *shared_parts(f))

            def gather(j, c):
                i, s = tile(j, c), c % RING
                pool.wait_ge(rows_out, 16 * 2)
                pool.wait_ge(gather_id_done, i + 1)
                if has(i, RING):
                    pool.wait_ge(hg_ready, i - (RING - 1))
                    pool.wait_ge(w_done, i - (RING - 1))
                pool.sem_inc(pool_clear, 1)
                nc.gpsimd.indirect_dma_start(rows[:, s, :], None, h_rows,
                                             bass.IndirectOffsetOnAxis(ap=gather_id[:, s:s + 1], axis=0)
                                             ).then_inc(rows_in[s], 16)

            def add(j, c):
                i, s, b = tile(j, c), c % RING, c % 2
                pool.wait_ge(sums_zero, 16 * 2)
                pool.wait_ge(y_copied, i + 1)
                pool.wait_ge(add_id_done, i + 1)
                if has(i, 2):
                    pool.wait_ge(added[b], turn(j, c) * 16)
                pool.sem_inc(pool_clear, 1)
                nc.gpsimd.indirect_dma_start(sums[b], bass.IndirectOffsetOnAxis(ap=add_id[:, s:s + 1], axis=0),
                                             y[:, s, :], None, compute_op=ALU.add).then_inc(added[b], 16)

            behind = 5
            for i in range(2 * RING):
                gather(0, i)
                if i >= behind:
                    add(0, i - behind)
            with pool.Fori(0, LAPS - 1) as j:
                for b in range(RING):
                    gather(j, 2 * RING + b)
                    add(j, 2 * RING + b - behind)
            for i in range(RING * (LAPS + 1), TILES):
                gather(0, i)
                add(0, i - behind)
            for i in range(TILES - behind, TILES):
                add(0, i)

        @block.scalar
        def _(act):
            act.dma_start(cond_w_sb[:], cond_w.rearrange("(k p) d -> p k d", p=P)).then_inc(cond_in, 16)
            for k in range(KD):
                act.dma_start(cond_b_sb[:, k, :, :],
                              cond_b[:, k * P:(k + 1) * P, :].rearrange("a p r -> p a r")).then_inc(cond_in, 16)
            act.dma_start(shw_sb[:], sh_gate_w.rearrange("(k p) o -> p k o", p=P),
                          allow_slow_non_contiguous=True).then_inc(small_in, 16)
            act.dma_start(idx_sb[:], adapter_idx.rearrange("(a b) -> a b", a=1).to_broadcast([P, B])).then_inc(small_in, 16)
            act.dma_start(scale_sb[:], scalings.rearrange("(a o) -> a o", o=1).unsqueeze(1)
                          .to_broadcast([NA, RANK, 1]), allow_slow_non_contiguous=True).then_inc(small_in, 16)

            def x_high(t):
                for k in range(KD):
                    act.wait_ge(xT_ready, t * KD + k + 1)
                    nc.scalar.activation(xT_hi[:, k, t * HALF:(t + 1) * HALF], acc[k][t][:, :],
                                         ACT.Copy).then_inc(x_hi_done, 1)

            x_high(0)
            for j, ps in enumerate((abT_ps, wT_ps)):
                act.wait_ge(condT_ready, j + 1)
                nc.scalar.activation(condT_hi[:, 4 * j:4 * j + 4, :].rearrange("p b c -> p (b c)"), ps[:, :],
                                     ACT.Copy).then_inc(cond_hi_done, 1)
            x_high(1)
            act.wait_ge(gates_w_done, 3)
            nc.scalar.activation(gates_hi[:], gates_w[:], ACT.Copy).then_inc(gates_hi_done, 1)

            def high_parts(gu, dn):
                for _, dst, raw in gu:
                    last = nc.scalar.activation(dst, raw, ACT.Copy)
                last.then_inc(wgu_hi_done, 1)
                for _, dst, raw in dn:
                    last = nc.scalar.activation(dst, raw, ACT.Copy)
                last.then_inc(wdn_hi_done, 1)

            for t in range(NH):
                cols = slice(t * HALF, (t + 1) * HALF)
                act.wait_ge(xa_done, t + 1)
                if t:
                    act.wait_ge(h_ready, t * KD)
                nc.scalar.activation(xa_hi[:], xa[:], ACT.Copy).then_inc(xa_hi_done, 1)
                if t:
                    act.wait_ge(shared_in, 16 * 4)
                    high_parts(*shared_parts(0))
                for o in range(KD):
                    act.wait_ge(h_ready, t * KD + o + 1)
                    nc.scalar.activation(hT_hi[:, o, cols], h_ps[o][t][:, :], ACT.Copy).then_inc(h_hi_done, 1)
                for o in range(KD):
                    act.wait_ge(h_lo_done, t * KD + o + 1)
                    nc.scalar.activation(hT[:, o, cols], h_ps[o][t][:, :], ACT.Copy).then_inc(hT_done, 1)
            def copy_logits(t):
                act.wait_ge(gates_ready, t + 1)
                nc.scalar.activation(logitsT[:, t * HALF:(t + 1) * HALF], gates_ps[t][0:LG, :],
                                     ACT.Copy).then_inc(logits_copied, 1)

            def exponentials():
                act.wait_ge(tok_ready, 1)
                nc.scalar.activation(sg[:], tok_ps[:, 0:NT * LG].rearrange("p (n e) -> p n e", e=LG)[:, :, E],
                                     ACT.Tanh, scale=0.5).then_inc(tanh_done, 1)
                act.wait_ge(shifted_done, 1)
                nc.scalar.activation(expd[:], shifted[:], ACT.Exp).then_inc(exp_done, 1)

            def copy_rows():
                for q in range(NT // 2):
                    act.wait_ge(hrow_ready, q + 1)
                    nc.scalar.activation(h_row[:, 2 * q:2 * q + 2, 0:D],
                                         hrow_ps[q][:, :].rearrange("p (n d) -> p n d", d=D),
                                         ACT.Copy).then_inc(hrow_copied, 1)

            def gate_half(f, t, rows=P):
                n = unit_of(f, t)
                act.wait_ge(gate_ready if rows == P else up_ready, n + 1)
                if not (isinstance(n, int) and n < NH):
                    act.wait_ge(inner_done, n - (NH - 1))
                nc.scalar.activation(silu[0:rows, t, :], gate_ps[t][0:rows, :], ACT.Silu).then_inc(silu_done, 1)

            def high_half(f, t, rows=P):
                n = unit_of(f, t)
                act.wait_ge(inner_done, n + 1)
                if not (isinstance(n, int) and n < NH):
                    act.wait_ge(down_done, n - (NH - 1))
                nc.scalar.activation(inner_hi[0:rows, t, :], inner[0:rows, t, :],
                                     ACT.Copy).then_inc(inner_hi_done, 1)

            def chunk(f, parts, rows=P):
                if f == 0:
                    copy_logits(0)
                gate_half(f, 0, rows)
                high_half(f, 0, rows)
                if f == 0:
                    copy_logits(1)
                if parts:
                    gu, dn = parts
                    first = isinstance(f, int) and f == 0
                    if not first:
                        act.wait_ge(up_ready, unit_of(f, 0))
                    for _, dst, raw in gu:
                        last = nc.scalar.activation(dst, raw, ACT.Copy)
                    last.then_inc(wgu_hi_done, 1)
                gate_half(f, 1, rows)
                if f == 0:
                    exponentials()
                    copy_rows()
                if parts:
                    if not first:
                        act.wait_ge(down_done, unit_of(f, 0))
                    for _, dst, raw in dn:
                        last = nc.scalar.activation(dst, raw, ACT.Copy)
                    last.then_inc(wdn_hi_done, 1)
                high_half(f, 1, rows)

            def copy_hg(j, c):
                i, b = tile(j, c), c % 2
                act.wait_ge(hg_ready, i + 1)
                if has(i, 2):
                    act.wait_ge(rgu_ready, i - 1)
                nc.scalar.activation(hgT[:, b, :, :].rearrange("p k s -> p (k s)"), hg_ps[b][:, 0:KD * P],
                                     ACT.Copy).then_inc(hg_copied, 1)

            for f in range(SHARED):
                chunk(f, shared_parts(f + 1) if f + 1 < SHARED else None, P if f < SF else SR)
            copy_hg(0, 0)
            for t in range(NH):
                act.wait_ge(down_done, unit_of(SHARED - 1, t) + 1)
                nc.scalar.activation(sharedT[:, 0, t * HALF:(t + 1) * HALF], acc[0][t][:, :],
                                     ACT.Copy).then_inc(accT_a, 1)

            def silu_tile(j, c):
                i, b = tile(j, c), c % 2
                act.wait_ge(rgu_ready, i + 1)
                if has(i, 2):
                    act.wait_ge(r_inner_done, i - 1)
                nc.scalar.activation(r_silu[:, b, :], rgu_ps[b][:, 0:I], ACT.Silu).then_inc(r_silu_done, 1)

            def copy_y(j, c):
                i, s, b = tile(j, c), c % RING, c % 2
                act.wait_ge(y_ready, i + 1)
                if has(i, RING):
                    act.wait_ge(added[b], (turn(j, c) - (RING // 2 - 1)) * 16)
                nc.scalar.activation(y[:, s, :], y_ps[b][:, 0:D], ACT.Copy).then_inc(y_copied, 1)

            def copy_innerT(j, c):
                i, b = tile(j, c), c % 2
                act.wait_ge(innerT_ready, i + 1)
                if has(i, 2):
                    act.wait_ge(y_ready, i - 1)
                nc.scalar.activation(innerT[:, b, 0, :], innerT_ps[b][:, 0:P], ACT.Copy)
                nc.scalar.activation(innerT[0:IR, b, 1, :], innerT_ps[b][0:IR, P:2 * P],
                                     ACT.Copy).then_inc(innerT_copied, 1)

            for i in range(4):
                silu_tile(0, i)
                copy_hg(0, i + 1)
                if i >= 2:
                    copy_y(0, i - 2)
                if i >= 1:
                    copy_innerT(0, i - 1)
            with act.Fori(0, LAPS) as j:
                for c in range(4, 4 + RING):
                    silu_tile(j, c)
                    copy_hg(j, c + 1)
                    copy_y(j, c - 2)
                    copy_innerT(j, c - 1)
            for i in range(TILES - 3, TILES):
                silu_tile(0, i)
                if i + 1 < TILES:
                    copy_hg(0, i + 1)
                copy_y(0, i - 2)
                copy_innerT(0, i - 1)
            copy_y(0, TILES - 2)
            copy_innerT(0, TILES - 1)
            copy_y(0, TILES - 1)

        @block.vector
        def _(dve):
            steps = [0]

            def step(ins):
                steps[0] += 1
                ins.then_inc(dve_step, 1)
                dve.wait_ge(dve_step, steps[0])

            def x_low(t):
                for k in range(KD):
                    cols = slice(t * HALF, (t + 1) * HALF)
                    dve.wait_ge(x_hi_done, t * KD + k + 1)
                    nc.vector.tensor_tensor(xT_lo[:, k, cols], acc[k][t][:, :], xT_hi[:, k, cols].bitcast(F32),
                                            ALU.subtract).then_inc(x_lo_done, 1)

            x_low(0)
            for j, ps in enumerate((abT_ps, wT_ps)):
                dve.wait_ge(cond_hi_done, j + 1)
                blocks = slice(4 * j, 4 * j + 4)
                nc.vector.tensor_tensor(condT_lo[:, blocks, :].rearrange("p b c -> p (b c)"), ps[:, :],
                                        condT_hi[:, blocks, :].rearrange("p b c -> p (b c)").bitcast(F32),
                                        ALU.subtract).then_inc(cond_lo_done, 1)
                if j == 0:
                    dve.wait_ge(routerT_ready, 1)
                    dve.wait_ge(gates_w_done, 1)
                    nc.vector.tensor_copy(gates_w[:, :, 0:E], routerT_ps[:, 0:KD * E]
                                          .rearrange("p (k e) -> p k e", e=E)).then_inc(gates_w_done, 1)
                    dve.wait_ge(small_in, 16 * 3)
                    nc.vector.tensor_copy(gates_w[:, :, E:E + 1], shw_sb[:]).then_inc(gates_w_done, 1)
            dve.wait_ge(pool_step, 3)
            step(nc.vector.tensor_single_scalar(part_a[:], part_i[:], RANK.bit_length() - 1, ALU.arith_shift_right))
            step(nc.vector.tensor_copy(adapter_of_part[:], part_a[:]))
            step(nc.vector.tensor_copy(idx_f[:], idx_sb[:]))
            step(nc.vector.tensor_scalar(adapter_coef[:], idx_f[:], adapter_of_part[:, 0:1], scale_sb[:, 0:1],
                                         ALU.is_equal, ALU.mult))
            for t in range(NH):
                dve.wait_ge(xa_ready, t + 1)
                if t:
                    dve.wait_ge(xa_lo_done, t)
                    dve.wait_ge(xa_hi_done, t)
                nc.vector.tensor_tensor(
                    xa[:].rearrange("p (b t) -> p b t", t=T), xa_ps[t][:, :].rearrange("p (b t) -> p b t", t=T),
                    adapter_coef[:, t * BH:(t + 1) * BH].unsqueeze(2).to_broadcast([P, BH, T]),
                    ALU.mult).then_inc(xa_done, 1)
                dve.wait_ge(xa_hi_done, t + 1)
                nc.vector.tensor_tensor(xa_lo[:], xa[:], xa_hi[:].bitcast(F32), ALU.subtract).then_inc(xa_lo_done, 1)
                if t == 0:
                    x_low(1)
                    dve.wait_ge(gates_hi_done, 1)
                    nc.vector.tensor_tensor(gates_lo[:], gates_w[:], gates_hi[:].bitcast(F32),
                                            ALU.subtract).then_inc(gates_lo_done, 1)
                for o in range(KD):
                    cols = slice(t * HALF, (t + 1) * HALF)
                    dve.wait_ge(h_hi_done, t * KD + o + 1)
                    nc.vector.tensor_tensor(hT_lo[:, o, cols], h_ps[o][t][:, :], hT_hi[:, o, cols].bitcast(F32),
                                            ALU.subtract).then_inc(h_lo_done, 1)
            def over_experts(v):
                return v[:].unsqueeze(2).to_broadcast([P, NT, E])

            def softmax():
                tok = tok_ps[:, 0:NT * LG].rearrange("p (n e) -> p n e", e=LG)[:, :, 0:E]
                dve.wait_ge(tok_ready, 1)
                dve.wait_ge(tanh_done, 1)
                step(nc.vector.tensor_reduce(mx[:], tok, AX_X, ALU.max))
                nc.vector.tensor_tensor(shifted[:], tok, over_experts(mx), ALU.subtract).then_inc(shifted_done, 1)
                nc.vector.tensor_scalar(sg[:], sg[:], 0.5, 0.5, ALU.mult, ALU.add).then_inc(sg_done, 1)
                dve.wait_ge(exp_done, 1)
                step(nc.vector.tensor_reduce(den[:], expd[:], AX_X, ALU.add))
                step(nc.vector.reciprocal(rden[:], den[:]))
                step(nc.vector.tensor_tensor(probs[:], expd[:], over_experts(rden), ALU.mult))

            def multiply(f, t, rows=P, up_src=None):
                n = unit_of(f, t)
                dve.wait_ge(up_ready, n + 1)
                dve.wait_ge(silu_done, n + 1)
                if n >= NH:
                    dve.wait_ge(inner_hi_done, n - (NH - 1))
                    dve.wait_ge(inner_lo_done, n - (NH - 1))
                nc.vector.tensor_tensor(inner[0:rows, t, :], up_ps[t][:, :] if up_src is None else up_src,
                                        silu[0:rows, t, :], ALU.mult).then_inc(inner_done, 1)

            def low_part(f, t, rows=P):
                n = unit_of(f, t)
                dve.wait_ge(inner_hi_done, n + 1)
                nc.vector.tensor_tensor(inner_lo[0:rows, t, :], inner[0:rows, t, :],
                                        inner_hi[0:rows, t, :].bitcast(F32),
                                        ALU.subtract).then_inc(inner_lo_done, 1)

            def choose():
                for n in range(NT):
                    last = nc.vector.max(top[:, n, :], probs[:, n, :])
                step(last)
                for n in range(NT):
                    last = nc.vector.max_index(top_i[:, n, :], top[:, n, :], probs[:, n, :])
                step(last)

            def weigh():
                step(nc.vector.tensor_copy(top_f[:], top_i[:]))
                step(nc.vector.tensor_tensor(
                    hit[:], experts[:].unsqueeze(1).unsqueeze(1).to_broadcast([P, NT, TOP_K, E]),
                    top_f[:, :, 0:TOP_K].unsqueeze(3).to_broadcast([P, NT, TOP_K, E]), ALU.is_equal))
                step(nc.vector.tensor_reduce(picked[:], hit[:].rearrange("p n k e -> p n e k"), AX_X, ALU.add))
                nc.vector.tensor_copy(picked_b[:], picked[:]).then_inc(picked_done, 1)
                step(nc.vector.tensor_reduce(topsum[:], top[:, :, 0:TOP_K], AX_X, ALU.add))
                step(nc.vector.tensor_scalar(topsum[:], topsum[:], 1e-9, None, ALU.max))
                step(nc.vector.reciprocal(rtop[:], topsum[:]))
                step(nc.vector.tensor_tensor(kept[:], picked[:], probs[:], ALU.mult))
                nc.vector.tensor_tensor(h_row[:, :, D:ROW], kept[:], over_experts(rtop), ALU.mult).then_inc(comb_done, 1)

            def take_counts():
                dve.wait_ge(count_ready, 1)
                nc.vector.tensor_copy(counts[:], count_ps[:, 0:NT * E + E]).then_inc(count_copied, 1)
                dve.wait_ge(count_copied, 1)

            def place_experts():
                step(nc.vector.tensor_scalar(tiles_i[:], counts[:, NT * E:], float(P - 1), None, ALU.add))
                step(nc.vector.tensor_single_scalar(tiles_s[:], tiles_i[:], P.bit_length() - 1, ALU.arith_shift_right))
                step(nc.vector.tensor_copy(tiles_f[:], tiles_s[:]))
                dve.wait_ge(pool_step, 8)
                step(nc.vector.tensor_tensor(tiles_b[:], below[:], tiles_f[:].unsqueeze(1).to_broadcast([P, E, E]),
                                             ALU.mult))
                step(nc.vector.tensor_reduce(begin[:], tiles_b[:], AX_X, ALU.add))
                step(nc.vector.tensor_tensor(end[:], begin[:], tiles_f[:], ALU.add))
                step(nc.vector.scalar_tensor_tensor(
                    out=slot_e[:], in0=begin[:].unsqueeze(1).to_broadcast([P, NT, E]), scalar=float(P),
                    in1=counts[:, 0:NT * E].rearrange("p (n e) -> p n e", e=E), op0=ALU.mult, op1=ALU.add))
                step(nc.vector.tensor_tensor(hit[:], hit[:],
                                             slot_e[:].unsqueeze(2).to_broadcast([P, NT, TOP_K, E]), ALU.mult))
                step(nc.vector.tensor_reduce(slot_k[:], hit[:], AX_X, ALU.add))
                step(nc.vector.tensor_copy(slot_i[:], slot_k[:]))
                step(nc.vector.tensor_single_scalar(lane_i[:], slot_i[:], P - 1, ALU.bitwise_and))
                step(nc.vector.tensor_single_scalar(tile_i[:], slot_i[:], P.bit_length() - 1, ALU.arith_shift_right))
                nc.vector.tensor_copy(tile_f[:], tile_i[:]).then_inc(tile_f_done, 1)
                step(nc.vector.tensor_copy(lane_f[:], lane_i[:]))

            def one_hot(n):
                dve.wait_ge(pool_step, 12)
                for k in range(TOP_K):
                    last = nc.vector.tensor_scalar(lane_hot[:, n, k, :], lanes[:], lane_f[:, n, k:k + 1], None,
                                                   ALU.is_equal)
                    if n % 2:
                        last = nc.vector.tensor_scalar(tile_hot[:, n, k, :], tiles[:], tile_f[:, n, k:k + 1],
                                                       token1[:, n:n + 1], ALU.is_equal, ALU.mult)
                last.then_inc(hot_done, 1)

            def take_tokens():
                dve.wait_ge(token_ready, 1)
                step(nc.vector.tensor_scalar(vacant[:], token_ps[:, 0:TILES], 0.0, empty1[:, 0:1],
                                             ALU.is_equal, ALU.mult))
                nc.vector.scalar_tensor_tensor(out=slot_token[:], in0=token_ps[:, 0:TILES], scalar=-1.0,
                                               in1=vacant[:], op0=ALU.add, op1=ALU.add).then_inc(token_done, 1)
                dve.wait_ge(token_done, 1)
                for i in range(RING):
                    nc.vector.tensor_copy(gather_id[:, i:i + 1], slot_token[:, i:i + 1]).then_inc(gather_id_done, 1)

            def begun_ended():
                number = tiles[:].unsqueeze(2).to_broadcast([P, TILES, E])
                nc.vector.tensor_tensor(begun[:], number, begin[:].unsqueeze(1).to_broadcast([P, TILES, E]), ALU.is_ge)
                nc.vector.tensor_tensor(ended[:], number, end[:].unsqueeze(1).to_broadcast([P, TILES, E]),
                                        ALU.is_ge).then_inc(ended_done, 1)

            def place_tiles():
                dve.wait_ge(ended_done, 1)
                step(nc.vector.tensor_reduce(expert_f[:], ended[0:1, :, :], AX_X, ALU.add))
                nc.vector.tensor_scalar(expert_of[:], expert_f[:], float(E - 1), None, ALU.min).then_inc(expert_done, 1)
                step(nc.vector.tensor_tensor(begun[:], begun[:], ended[:], ALU.subtract))

            between = {(0, 1): [softmax], (1, 1): [take_counts], (4, 0): [begun_ended]}
            behind = {(0, 1): [choose, weigh], (1, 1): [place_experts], (3, 1): [take_tokens], (4, 0): [place_tiles]}
            for f in range(SHARED):
                for t in range(NH):
                    if f < SF:
                        multiply(f, t)
                    else:
                        multiply(f, t, SR, gate_ps[t][SR:2 * SR, :])
                    for work in between.get((f, t), ()):
                        work()
                    if f in (2, 3):
                        one_hot(2 * unit_of(f - 2, t))
                    low_part(f, t, P if f < SF else SR)
                    if f in (2, 3):
                        one_hot(2 * unit_of(f - 2, t) + 1)
                    for work in behind.get((f, t), ()):
                        work()
            for t in range(NH):
                dve.wait_ge(down_done, unit_of(SHARED - 1, t) + 1)
                nc.vector.tensor_copy(sharedT[:, 1, t * HALF:(t + 1) * HALF], acc[1][t][:, :]).then_inc(accT_v, 1)
            def add_shared(q):
                for n in (2 * q, 2 * q + 1):
                    dve.wait_ge(outT_ready, q + 1)
                    nc.vector.scalar_tensor_tensor(out=x_sb[:, n, :], in0=hrow_ps[q][:, n % 2 * D:(n % 2 + 1) * D],
                                                   scalar=sg[:, n:n + 1], in1=x_sb[:, n, :], op0=ALU.mult,
                                                   op1=ALU.add).then_inc(base_done, 1)

            def one(v, i):
                return v[:, bass.ds(i, 1)]

            def weight_slots(j, c):
                i, s, b = tile(j, c), c % RING, c % 2
                dve.wait_ge(rows_in[s], lap(j, c) * 16 + 16)
                nc.vector.tensor_tensor(w_e[:, b, :], rows[:, s, D:ROW],
                                        begun[:, bass.ds(i, 1), :].rearrange("p o e -> p (o e)"),
                                        ALU.mult).then_inc(w_part, 1)
                dve.wait_ge(w_part, i + 1)
                nc.vector.tensor_reduce(w_slot[:, s:s + 1], w_e[:, b, :], AX_X, ALU.add).then_inc(w_done, 1)

            def inner_tile(j, c):
                i, s, b = tile(j, c), c % RING, c % 2
                dve.wait_ge(w_done, i + 1)
                dve.wait_ge(r_silu_done, i + 1)
                if has(i, 2):
                    dve.wait_ge(innerT_ready, i - 1)
                nc.vector.scalar_tensor_tensor(out=r_inner[:, b, :], in0=rgu_ps[b][:, I:2 * I],
                                               scalar=w_slot[:, s:s + 1], in1=r_silu[:, b, :],
                                               op0=ALU.mult, op1=ALU.mult).then_inc(r_inner_done, 1)

            def next_gather(j, c):
                i, s = tile(j, c), c % RING
                dve.wait_ge(rows_in[s], lap(j, c) * 16)
                nc.vector.tensor_copy(gather_id[:, s:s + 1], one(slot_token, i)).then_inc(gather_id_done, 1)

            def next_add(j, c):
                i, s, b = tile(j, c), c % RING, c % 2
                if has(i, RING):
                    dve.wait_ge(added[b], (turn(j, c) - (RING // 2 - 1)) * 16)
                nc.vector.tensor_copy(add_id[:, s:s + 1], one(slot_token, i)).then_inc(add_id_done, 1)

            def ahead(j, c, following=True):
                weight_slots(j, c)
                if following:
                    next_gather(j, c + RING)

            def dve_tile(j, c):
                inner_tile(j, c)
                next_add(j, c)

            ahead(0, 0)
            ahead(0, 1)
            for q in range(NT // 2):
                add_shared(q)
                if q == 0:
                    dve_tile(0, 0)
            for i in range(1, 4):
                ahead(0, i + 1)
                dve_tile(0, i)
            with dve.Fori(0, LAPS - 1) as j:
                for c in range(4, 4 + RING):
                    ahead(j, c + 1)
                    dve_tile(j, c)
            for i in range(RING * LAPS, TILES):
                if i + 1 < TILES:
                    ahead(0, i + 1, i + 1 + RING < TILES)
                dve_tile(0, i)
            for q in range(NT // 2):
                ts = slice(2 * q, 2 * q + 2)
                dve.wait_ge(sum_in[1][q], 16)
                nc.vector.tensor_tensor(x_sb[:, ts, :], sum_sb[1][:, ts, :], x_sb[:, ts, :], ALU.add).then_inc(sum_done, 1)
            for q in range(NT // 2):
                ts = slice(2 * q, 2 * q + 2)
                dve.wait_ge(sum_done, q + 1)
                dve.wait_ge(sum_in[0][q], 16)
                nc.vector.tensor_tensor(sum_sb[0][:, ts, :], sum_sb[0][:, ts, :], x_sb[:, ts, :],
                                        ALU.add).then_inc(out_done, 1)

        @block.tensor
        def _(pe):
            def product(dst, pairs, first=True, last=True, begun=None):
                terms = []
                for w_hi, w_lo, m_hi, m_lo in pairs:
                    terms += [(w_hi, m_hi), (w_hi, m_lo), (w_lo, m_hi)]
                for j, (w, m) in enumerate(terms):
                    mm = nc.tensor.matmul(dst, w, m, start=first and j == 0, stop=last and j == len(terms) - 1)
                    if j == 0 and begun is not None:
                        mm.then_inc(begun, 1)
                return mm

            pe.wait_ge(ident_ready, 1)
            for _ in range(WARM):
                nc.tensor.matmul(up_ps[1][:, 0:P], ident[:], ident[:], start=True, stop=True)

            def transpose_x(t):
                pe.wait_ge(x_in[t], 16)
                for k in range(KD):
                    for j in range(TPH):
                        mm = nc.tensor.transpose(acc[k][t][:, j * P:(j + 1) * P],
                                                 x_sb[:, t * TPH + j, k * P:(k + 1) * P], ident[:])
                    mm.then_inc(xT_ready, 1)

            transpose_x(0)
            pe.wait_ge(cond_in, 16 * (3 + KD))
            for k in range(KD):
                nc.tensor.transpose(abT_ps[:, k * P:(k + 1) * P], cond_a_sb[:, k * P:(k + 1) * P], ident[:])
            for o in range(KD):
                mm = nc.tensor.transpose(abT_ps[:, (KD + o) * P:(KD + o + 1) * P],
                                         cond_b_sb[:, o, :, :].rearrange("p a r -> p (a r)"), ident[:])
            mm.then_inc(condT_ready, 1)
            for k in range(KD):
                for o in range(KD):
                    mm = nc.tensor.transpose(wT_ps[:, (KD * k + o) * P:(KD * k + o + 1) * P],
                                             cond_w_sb[:, o, k * P:(k + 1) * P], ident[:])
            mm.then_inc(condT_ready, 1)
            for k in range(KD):
                mm = nc.tensor.transpose(routerT_ps[:, k * E:(k + 1) * E], router_sb[:, k * P:(k + 1) * P],
                                         ident[0:E, 0:E])
            mm.then_inc(routerT_ready, 1)
            transpose_x(1)

            def w_block(k, o):
                return condT_hi[:, 4 + KD * k + o, :], condT_lo[:, 4 + KD * k + o, :]

            def a_block(k):
                return condT_hi[:, k, :], condT_lo[:, k, :]

            def b_block(o):
                return condT_hi[:, KD + o, :], condT_lo[:, KD + o, :]

            for t in range(NH):
                cols = slice(t * HALF, (t + 1) * HALF)
                pe.wait_ge(cond_lo_done, 1)
                pe.wait_ge(x_lo_done, (t + 1) * KD)
                pe.wait_ge(gates_w_done, 3)
                product(xa_ps[t][:, :], [(*a_block(k), xT_hi[:, k, cols], xT_lo[:, k, cols])
                                         for k in range(KD)]).then_inc(xa_ready, 1)
                pe.wait_ge(cond_lo_done, 2)
                for o in range(KD):
                    product(h_ps[o][t][:, :], [(*w_block(k, o), xT_hi[:, k, cols], xT_lo[:, k, cols])
                                               for k in range(KD)], last=False)
                pe.wait_ge(xa_lo_done, t + 1)
                for o in range(KD):
                    mm = product(h_ps[o][t][:, :], [(*b_block(o), xa_hi[:], xa_lo[:])], first=False)
                    mm.then_inc(h_ready, 1)
            def gates(t):
                pe.wait_ge(gates_lo_done, 1)
                pe.wait_ge(h_lo_done, (t + 1) * KD)
                pe.wait_ge(hT_done, t * KD + 1)
                cols = slice(t * HALF, (t + 1) * HALF)
                product(gates_ps[t][0:LG, :], [(gates_hi[:, k, :], gates_lo[:, k, :], hT_hi[:, k, cols], hT_lo[:, k, cols])
                                               for k in range(KD)]).then_inc(gates_ready, 1)

            def transpose_logits():
                pe.wait_ge(logits_copied, NH)
                pe.wait_ge(hT_done, KD)
                for n in range(NT):
                    mm = nc.tensor.transpose(tok_ps[:, n * LG:(n + 1) * LG], logitsT[:, n * P:(n + 1) * P],
                                             ident[0:LG, 0:LG])
                mm.then_inc(tok_ready, 1)

            def transpose_h():
                for q in range(NT // 2):
                    if q == NT // 2 - 1:
                        pe.wait_ge(shifted_done, 1)
                    for j in range(2):
                        for k in range(KD):
                            mm = nc.tensor.transpose(hrow_ps[q][:, (j * KD + k) * P:(j * KD + k + 1) * P],
                                                     hT[:, k, (2 * q + j) * P:(2 * q + j + 1) * P], ident[:])
                    mm.then_inc(hrow_ready, 1)

            def gate_up(f, t, s, short=False):
                n = unit_of(f, t)
                cols = slice(t * HALF, (t + 1) * HALF)
                if t == 0:
                    pe.wait_ge(wgu_lo_done, f + 1)
                def operands(g):
                    return [(gu_hi[:, s, g, k, :], gu_lo[:, s, g, k, :], hT_hi[:, k, cols], hT_lo[:, k, cols])
                            for k in range(KD)]
                if n >= NH:
                    pe.wait_ge(inner_done, n - (NH - 1))
                if n < NH:
                    pe.wait_ge(xa_done, n + 1)
                if short:
                    product(gate_ps[t][:, :], operands(0), begun=gate_ready).then_inc(up_ready, 1)
                    return
                product(gate_ps[t][:, :], operands(0)).then_inc(gate_ready, 1)
                product(up_ps[t][:, :], operands(1)).then_inc(up_ready, 1)

            def down(f, t, s, first=False, last=False, rows=P):
                n = unit_of(f, t)
                if t == 0:
                    pe.wait_ge(wdn_lo_done, f + 1)
                pe.wait_ge(inner_lo_done, n + 1)
                for o in range(KD):
                    w = slice(o * P, (o + 1) * P)
                    mm = product(acc[o][t][:, :], [(dn_hi[0:rows, s, w], dn_lo[0:rows, s, w],
                                                    inner_hi[0:rows, t, :], inner_lo[0:rows, t, :])],
                                 first=first, last=last)
                mm.then_inc(down_done, 1)

            def count():
                pe.wait_ge(picked_done, 1)
                pe.wait_ge(pool_step, 8)
                for n in range(NT - 1):
                    behind = NT - 1 - n
                    nc.tensor.matmul(count_ps[:, (n + 1) * E:NT * E], ones[:],
                                     picked_b[:, n:n + 1, :].to_broadcast([P, behind, E]),
                                     start=n == 0, stop=False, skip_group_check=True)
                nc.tensor.matmul(count_ps[:, 0:NT * E], before[:], picked_b[:].rearrange("p n e -> p (n e)"),
                                 start=False, stop=True, skip_group_check=True)
                for n in range(NT):
                    mm = nc.tensor.matmul(count_ps[:, NT * E:NT * E + E], ones[:], picked_b[:, n, :],
                                          start=n == 0, stop=n == NT - 1, skip_group_check=True)
                mm.then_inc(count_ready, 1)

            def tabulate():
                for n in range(NT):
                    pe.wait_ge(hot_done, n + 1)
                    if n % 2 == 0:
                        pe.wait_ge(tile_hot_done, n // 2 + 1)
                    for k in range(TOP_K):
                        mm = nc.tensor.matmul(token_ps[:, 0:TILES], lane_hot[:, n, k, :], tile_hot[:, n, k, :],
                                              start=n == 0 and k == 0, stop=n == NT - 1 and k == TOP_K - 1)
                mm.then_inc(token_ready, 1)

            gates(0)
            gate_up(0, 0, slot_of(0))
            gates(1)
            gate_up(0, 1, slot_of(0))
            transpose_logits()
            pe.wait_ge(hT_done, NH * KD)
            transpose_h()
            for f in range(1, SHARED):
                short = f == SF
                rows_f = SR if short else P
                if f == 2:
                    pe.wait_ge(count_copied, 1)
                gate_up(f, 0, slot_of(f), short)
                if f == SF - 1:
                    pe.wait_ge(inner_done, unit_of(f, 0))
                    tabulate()
                if f == 1:
                    pe.wait_ge(hrow_copied, NT // 2)
                    down(0, 0, slot_of(0), first=True)
                down(f - 1, 1, slot_of(f - 1), first=f == 1)
                if f == SF - 1:
                    pe.wait_ge(token_done, 1)
                gate_up(f, 1, slot_of(f), short)
                if f == 1:
                    pe.wait_ge(inner_done, unit_of(f, 0) + 1)
                    count()
                if not short:
                    down(f, 0, slot_of(f))

            def transpose_shared():
                for q in range(NT // 2):
                    pe.wait_ge(accT_a, q // 2 + 1)
                    pe.wait_ge(accT_v, q // 2 + 1)
                    if q == 1:
                        pe.wait_ge(accT_a, NH)
                    for j in range(2):
                        n = 2 * q + j
                        for k in range(KD):
                            mm = nc.tensor.transpose(hrow_ps[q][:, (j * KD + k) * P:(j * KD + k + 1) * P],
                                                     sharedT[:, k, n * P:(n + 1) * P], ident[:])
                    mm.then_inc(outT_ready, 1)

            def transpose_rows(j, c):
                i, s, b = tile(j, c), c % RING, c % 2
                pe.wait_ge(rows_in[s], lap(j, c) * 16 + 16)
                for k in range(KD):
                    mm = nc.tensor.transpose(hg_ps[b][:, k * P:(k + 1) * P], rows[:, s, k * P:(k + 1) * P], ident[:])
                mm.then_inc(hg_ready, 1)

            def expert(i):
                return pe.value_load(expert_of[0:1, bass.ds(i, 1)], min_val=0, max_val=E - 1)

            def experts_of_lap(j):
                _, values = nc.values_load_multi_w_load_instructions(
                    expert_of[0:1, bass.ds(RING * j, 2 * RING)], engines=(mybir.EngineType.PE,),
                    min_val=0, max_val=E - 1, skip_runtime_bounds_check_because="place_tiles keeps them below E")
                return values

            def gate_up_tile(j, c, e):
                i, b = tile(j, c), c % 2
                pe.wait_ge(hg_copied, i + 1)
                if isinstance(i, int) and i < 2:
                    pe.wait_ge(inner_done, unit_of(SF, i) + 1)
                for k in range(KD):
                    w = routed_gu[:, k, bass.ds(e, 1), :].rearrange("p o c -> p (o c)")
                    mm = nc.tensor.matmul(rgu_ps[b][:, 0:2 * I], hgT[:, b, k, :], w, start=k == 0, stop=k == KD - 1)
                mm.then_inc(rgu_ready, 1)

            def transpose_inner(j, c):
                i, b = tile(j, c), c % 2
                pe.wait_ge(r_inner_done, i + 1)
                if isinstance(i, int) and i < 2:
                    pe.wait_ge(base_done, 2 * i + 2)
                nc.tensor.transpose(innerT_ps[b][:, 0:P], r_inner[:, b, 0:P], ident[:])
                nc.tensor.transpose(innerT_ps[b][0:IR, P:2 * P], r_inner[:, b, P:I],
                                    ident[:]).then_inc(innerT_ready, 1)

            def down_tile(j, c, e):
                i, b = tile(j, c), c % 2
                pe.wait_ge(innerT_copied, i + 1)
                if has(i, 2):
                    pe.wait_ge(y_copied, i - 1)
                else:
                    pe.wait_ge(base_done, NT)
                for q, rows_q in enumerate((P, IR)):
                    w = routed_d[0:rows_q, bass.ds(e, 1), q, :].rearrange("p o d -> p (o d)")
                    mm = nc.tensor.matmul(y_ps[b][:, 0:D], innerT[0:rows_q, b, q, :], w, start=q == 0, stop=q == 1)
                mm.then_inc(y_ready, 1)

            pe.wait_ge(expert_done, 1)
            for q in range(LOADS):
                pe.wait_ge(routed_in[q], 16 * (2 * KD + 2))
            transpose_rows(0, 0)
            down(SF, 0, slot_of(SF), last=True, rows=SR)
            gate_up_tile(0, 0, expert(0))
            down(SF, 1, slot_of(SF), last=True, rows=SR)
            transpose_rows(0, 1)
            transpose_shared()
            for i in range(1, 4):
                gate_up_tile(0, i, expert(i))
                transpose_rows(0, i + 1)
                if i >= 2:
                    down_tile(0, i - 2, expert(i - 2))
                transpose_inner(0, i - 1)
            with pe.Fori(0, LAPS) as j:
                e = experts_of_lap(j)
                for c in range(4, 4 + RING):
                    gate_up_tile(j, c, e[c])
                    transpose_rows(j, c + 1)
                    down_tile(j, c - 2, e[c - 2])
                    transpose_inner(j, c - 1)
            for i in range(TILES - 3, TILES):
                gate_up_tile(0, i, expert(i))
                if i + 1 < TILES:
                    transpose_rows(0, i + 1)
                down_tile(0, i - 2, expert(i - 2))
                transpose_inner(0, i - 1)
            down_tile(0, TILES - 2, expert(TILES - 2))
            transpose_inner(0, TILES - 1)
            down_tile(0, TILES - 1, expert(TILES - 1))


_INS = ['x', 'itok_B_0_6', 'L0_cond_W', 'L0_cond_A', 'L0_cond_Bm', 'L0_cond_scalings', 'L0_ffn_router_w',
        'L0_ffn_w_gate', 'L0_ffn_w_up', 'L0_ffn_w_down', 'L0_ffn_sh_gate', 'L0_ffn_sh_up', 'L0_ffn_sh_down',
        'L0_ffn_sh_gate_w']


def kernel(**inputs):
    import numpy as _np
    import concourse.bacc as _bacc
    from concourse import mybir as _mybir
    from concourse.bass_utils import run_bass_kernel_spmd as _run

    nc = _bacc.Bacc("TRN2", target_bir_lowering=False, num_devices=1)
    arrays, args = {}, []
    for name in _INS:
        a = _np.ascontiguousarray(inputs[name])
        arrays[f"in_{name}_dram"] = a
        args.append(nc.dram_tensor(f"in_{name}_dram", a.shape, _mybir.dt.from_np(a.dtype), kind="ExternalInput").ap())
    out = nc.dram_tensor("out_0_dram", inputs["x"].shape, _mybir.dt.float32, kind="ExternalOutput").ap()
    adaln_moe_ffn(nc, *args, out)
    r = _run(nc, [arrays], core_ids=[0])
    return r.results[0]["out_0_dram"]
```

```python
from contextlib import ExitStack

import concourse.bass as bass
from concourse import mybir

F32 = mybir.dt.float32
F32R = mybir.dt.float32r
I32 = mybir.dt.int32
U32 = mybir.dt.uint32
BF16 = mybir.dt.bfloat16
FP16 = mybir.dt.float16
ALU = mybir.AluOpType
ACT = mybir.ActivationFunctionType
AX_X = mybir.AxisListType.X

P = 128
HALF = 512
TOP_K = 4


def adaln_moe_ffn(nc, x, adapter_idx, cond_w, cond_a, cond_b, scalings, router_w, w_gate, w_up,
                  w_down, sh_gate, sh_up, sh_down, sh_gate_w, out):
    B, T, D = x.shape
    N = B * T
    NT = N // P
    KD = D // P
    NH = N // HALF
    TPH = HALF // P
    NA, RANK, _ = cond_a.shape
    E, _, I = w_gate.shape
    IS = sh_gate.shape[1]
    SF = IS // P
    SR = IS - SF * P
    SHARED = SF + 1
    TILES = (N * TOP_K - E) // P + E
    PAD = P
    ROW = D + E
    IR = I - P
    RING = 4
    LAPS = (TILES - 4 - 3) // RING
    WARM = 8
    ACT_WITHIN = {(0, 0): (0, 1), (0, 1): (2, 3), (1, 0): (5,), (1, 1): (6,), (2, 0): (7,), (2, 1): (11,),
                  (3, 0): (12,), (3, 1): (14,)}
    ACT_BEHIND = {(0, 1): (4,), (2, 0): (8, 9, 10), (3, 0): (13,), (3, 1): (15,)}
    DVE_WITHIN = {(0, 1): (2,), (4, 1): (12,), (5, 0): (14,)}
    DVE_BEHIND = {(0, 0): (0,), (4, 0): (11,)}
    POOL_LOWS, DVE_LOWS = 11, 5
    LG = 32
    LOADS = 4
    EL = E // LOADS
    LATE = 12
    assert NH == 2 and KD == 2 and NT == 8 and NA * RANK == P and 2 * SR == P and 0 < IR <= P == 1 << 7
    assert E == POOL_LOWS + DVE_LOWS == 16 and N * TOP_K <= TILES * P and TILES == RING * LAPS + 7
    assert NT * (ROW + 5 * E) <= (E - LATE) * KD * 2 * I
    BH = B // NH

    x_tok = x.rearrange("b t d -> (b t) d").rearrange("(n p) d -> p n d", p=P)
    out_tok = out[0:N, :].rearrange("(n p) d -> p n d", p=P)
    h_rows = nc.dram_tensor("h_rows", [N + PAD, ROW], F32, kind="Internal").ap()
    even_sums = nc.dram_tensor("even_sums", [N + PAD, D], F32, kind="Internal").ap()
    targets = [even_sums, out]

    with ExitStack() as ctx:
        def sb(name, shape, dt=F32, at=ctx):
            return at.enter_context(nc.sbuf_tensor(name, shape, dt))

        def f32(v):
            return v.bitcast(F32)

        def sem(name):
            return ctx.enter_context(nc.semaphore(name))

        x_sb = sb("x_sb", [P, NT, D])
        routed_d = sb("routed_d", [P, E, 2, D])
        with ExitStack() as raw:
            shared_gu = sb("shared_gu", [P, 2, KD, IS], at=raw)
            shared_d = sb("shared_d", [P, SF + 1, D], at=raw)
            routed_gu = sb("routed_gu", [P, E, KD, 2 * I], at=raw)
            silu = sb("silu", [P, 2, HALF], at=raw)
        shared_gu_lo = sb("shared_gu_lo", [P, 2, KD, IS], F32R)
        shared_d_lo = sb("shared_d_lo", [P, SF + 1, D], F32R)
        routed_gu_lo = sb("routed_gu_lo", [P, E, KD, 2 * I], F32R)
        inner_lo = sb("inner_lo", [P, 2, HALF], F32R)
        inner = silu

        with ExitStack() as passing:
            router_sb = sb("router_sb", [E, D], at=passing)
            shw_sb = sb("shw_sb", [P, KD, 1], at=passing)
            idx_sb = sb("idx_sb", [P, B], I32, at=passing)
            scale_sb = sb("scale_sb", [P, 1], at=passing)
            part_i = sb("part_i", [P, 1], I32, at=passing)
            part_a = sb("part_a", [P, 1], I32, at=passing)
            adapter_of_part = sb("adapter_of_part", [P, 1], at=passing)
            idx_f = sb("idx_f", [P, B], at=passing)
            adapter_coef = sb("adapter_coef", [P, B], at=passing)
            cond_w_sb = sb("cond_w_sb", [P, KD, D], at=passing)
            cond_a_sb = sb("cond_a_sb", [P, D], at=passing)
            cond_b_sb = sb("cond_b_sb", [P, KD, NA, RANK], at=passing)
            xT_hi = sb("xT_hi", [P, KD, N], F32R, at=passing)
            xT_lo = sb("xT_lo", [P, KD, N], F32R, at=passing)
            condT_hi = sb("condT_hi", [P, 8, P], F32R, at=passing)
            condT_lo = sb("condT_lo", [P, 8, P], F32R, at=passing)
            xa = sb("xa", [P, HALF], at=passing)
            xa_hi = sb("xa_hi", [P, HALF], F32R, at=passing)
            xa_lo = sb("xa_lo", [P, HALF], F32R, at=passing)
            gates_w = sb("gates_w", [P, KD, LG], at=passing)
            gates_hi = sb("gates_hi", [P, KD, LG], F32R, at=passing)
            gates_lo = sb("gates_lo", [P, KD, LG], F32R, at=passing)
        with ExitStack() as passing:
            sb("first_experts", [P, LATE, KD, 2 * I], at=passing)
            h_row = sb("h_row", [P, NT, ROW], at=passing)
            shifted = sb("shifted", [P, NT, E], at=passing)
            expd = sb("expd", [P, NT, E], at=passing)
            probs = sb("probs", [P, NT, E], at=passing)
            picked = sb("picked", [P, NT, E], at=passing)
            kept = sb("kept", [P, NT, E], at=passing)
        routed_gu_hi = sb("routed_gu_hi", [P, E, KD, 2 * I], F32R)

        hT = sb("hT", [P, KD, N])
        hT_hi = sb("hT_hi", [P, KD, N], F32R)
        hT_lo = sb("hT_lo", [P, KD, N], F32R)
        ident = sb("ident", [P, P])
        zeros = sb("zeros", [P, ROW])
        before = sb("before", [P, P], BF16)
        ones = sb("ones", [P, P], BF16)
        below = sb("below", [P, E, E])
        experts = sb("experts", [P, E])
        lanes = sb("lanes", [P, P], BF16)
        tiles = sb("tiles", [P, TILES], FP16)
        token1 = sb("token1", [P, NT])
        empty1 = sb("empty1", [P, 1])
        gu_hi = sb("gu_hi", [P, 2, 2, KD, P], F32R)
        dn_hi = sb("dn_hi", [P, 2, D], F32R)
        short_lo = sb("short_lo", [P, KD, P], F32R)
        inner_hi = sb("inner_hi", [P, 2, HALF], F32R)
        sg = sb("sg", [P, NT])
        vacant = sb("vacant", [P, TILES])
        slot_token = sb("slot_token", [P, TILES], U32)
        expert_f = sb("expert_f", [P, TILES])
        expert_of = sb("expert_of", [1, TILES], I32)
        tile_expert = sb("tile_expert", [P, TILES, E], BF16)
        gather_id = sb("gather_id", [P, RING], U32)
        add_id = sb("add_id", [P, RING], U32)
        with ExitStack() as routing:
            with ExitStack() as logits:
                logitsT = sb("logitsT", [LG, N], at=logits)
            lane_hot = sb("lane_hot", [P, NT, TOP_K, P], BF16, at=routing)
            tile_hot = sb("tile_hot", [P, NT, TOP_K, TILES], FP16, at=routing)
            mx = sb("mx", [P, NT], at=routing)
            den = sb("den", [P, NT], at=routing)
            rden = sb("rden", [P, NT], at=routing)
            top = sb("top", [P, NT, 8], at=routing)
            top_i = sb("top_i", [P, NT, 8], U32, at=routing)
            top_f = sb("top_f", [P, NT, 8], at=routing)
            hit = sb("hit", [P, NT, TOP_K, E], at=routing)
            picked_b = sb("picked_b", [P, NT, E], BF16, at=routing)
            topsum = sb("topsum", [P, NT], at=routing)
            rtop = sb("rtop", [P, NT], at=routing)
            counts = sb("counts", [P, NT * E + E], at=routing)
            tiles_i = sb("tiles_i", [P, E], I32, at=routing)
            tiles_s = sb("tiles_s", [P, E], I32, at=routing)
            tiles_f = sb("tiles_f", [P, E], at=routing)
            slot_e = sb("slot_e", [P, NT, E], at=routing)
            slot_k = sb("slot_k", [P, NT, TOP_K], at=routing)
            slot_i = sb("slot_i", [P, NT, TOP_K], I32, at=routing)
            lane_i = sb("lane_i", [P, NT, TOP_K], I32, at=routing)
            tile_i = sb("tile_i", [P, NT, TOP_K], I32, at=routing)
            lane_f = sb("lane_f", [P, NT, TOP_K], at=routing)
            tile_f = sb("tile_f", [P, NT, TOP_K], at=routing)
            begin = sb("begin", [P, E], at=routing)
            end = sb("end", [P, E], FP16, at=routing)
            ended = sb("ended", [P, TILES, E], BF16, at=routing)
        rows = sb("rows", [P, RING, ROW])
        w_e = sb("w_e", [P, 2, E])
        w_slot = sb("w_slot", [P, RING])
        hg_hi = sb("hg_hi", [P, 2, KD, P], F32R)
        hg_lo = sb("hg_lo", [P, 2, KD, P], F32R)
        r_silu = sb("r_silu", [P, 2, I])
        r_inner = sb("r_inner", [P, 2, I])
        innerT = sb("innerT", [P, 2, 2, P])
        y = sb("y", [P, RING, D])
        sharedT = hT
        acc = [[ctx.enter_context(nc.psum_tensor(f"acc_{o}_{t}", [P, HALF], F32)) for t in range(NH)]
               for o in range(KD)]
        gate_ps = [ctx.enter_context(nc.psum_tensor(f"gate_ps{t}", [P, HALF], F32)) for t in range(NH)]
        up_ps = [ctx.enter_context(nc.psum_tensor(f"up_ps{t}", [P, HALF], F32)) for t in range(NH)]
        wT_ps, abT_ps = gate_ps[0], gate_ps[1]
        routerT_ps = up_ps[1]
        xa_ps = [up_ps[0], up_ps[1]]
        h_ps = acc
        gates_ps = [acc[0][0], acc[0][1]]
        tok_ps = acc[1][0]
        hrow_ps = [acc[0][0], acc[0][1], acc[1][1], acc[1][0]]
        count_ps = gate_ps[1]
        token_ps = gate_ps[0]
        rgu_ps = gate_ps
        hg_ps = up_ps
        innerT_ps = acc[0]
        y_ps = acc[1]

        x_in = [sem(f"x_in{t}") for t in range(NH)]
        cond_in = sem("cond_in")
        small_in = sem("small_in")
        shared_in = sem("shared_in")
        routed_in = [sem(f"routed_in{q}") for q in range(LOADS)]
        routed_d_in = sem("routed_d_in")
        ident_ready = sem("ident_ready")
        pool_step = sem("pool_step")
        condT_ready = sem("condT_ready")
        routerT_ready = sem("routerT_ready")
        xT_ready = sem("xT_ready")
        cond_hi_done = sem("cond_hi_done")
        cond_lo_done = sem("cond_lo_done")
        x_hi_done = sem("x_hi_done")
        x_lo_done = sem("x_lo_done")
        gates_w_done = sem("gates_w_done")
        gates_hi_done = sem("gates_hi_done")
        gates_lo_done = sem("gates_lo_done")
        xa_ready = sem("xa_ready")
        xa_done = sem("xa_done")
        xa_hi_done = sem("xa_hi_done")
        xa_lo_done = sem("xa_lo_done")
        h_ready = sem("h_ready")
        h_hi_done = sem("h_hi_done")
        h_lo_done = sem("h_lo_done")
        gates_ready = sem("gates_ready")
        logits_copied = sem("logits_copied")
        tanh_done = sem("tanh_done")
        sg_done = sem("sg_done")
        tok_ready = sem("tok_ready")
        shifted_done = sem("shifted_done")
        exp_done = sem("exp_done")
        dve_step = sem("dve_step")
        hT_done = sem("hT_done")
        hrow_ready = sem("hrow_ready")
        hrow_copied = sem("hrow_copied")
        zeros_done = sem("zeros_done")
        picked_done = sem("picked_done")
        count_ready = sem("count_ready")
        count_copied = sem("count_copied")
        tile_f_done = sem("tile_f_done")
        routed_hi_done = sem("routed_hi_done")
        routed_lo_pool = sem("routed_lo_pool")
        routed_lo_dve = sem("routed_lo_dve")
        ended_done = sem("ended_done")
        hot_done = sem("hot_done")
        tile_hot_done = sem("tile_hot_done")
        token_ready = sem("token_ready")
        token_done = sem("token_done")
        expert_done = sem("expert_done")
        rows_out = sem("rows_out")
        sums_zero = sem("sums_zero")
        base_stored = sem("base_stored")
        rows_in = [sem(f"rows_in{b}") for b in range(RING)]
        added = [sem(f"added{b}") for b in range(2)]
        pool_clear = sem("pool_clear")
        gather_id_done = sem("gather_id_done")
        add_id_done = sem("add_id_done")
        w_part = sem("w_part")
        w_done = sem("w_done")
        hg_ready = sem("hg_ready")
        hg_hi_done = sem("hg_hi_done")
        hg_lo_done = sem("hg_lo_done")
        rgu_ready = sem("rgu_ready")
        r_silu_done = sem("r_silu_done")
        r_inner_done = sem("r_inner_done")
        innerT_ready = sem("innerT_ready")
        innerT_copied = sem("innerT_copied")
        y_ready = sem("y_ready")
        y_copied = sem("y_copied")
        base_done = sem("base_done")
        comb_done = sem("comb_done")
        wgu_hi_done = sem("wgu_hi_done")
        wgu_lo_done = sem("wgu_lo_done")
        wdn_hi_done = sem("wdn_hi_done")
        wdn_lo_done = sem("wdn_lo_done")
        gate_ready = sem("gate_ready")
        up_ready = sem("up_ready")
        silu_done = sem("silu_done")
        inner_done = sem("inner_done")
        inner_hi_done = sem("inner_hi_done")
        inner_lo_done = sem("inner_lo_done")
        down_done = sem("down_done")
        accT_a = sem("accT_a")
        accT_v = sem("accT_v")
        outT_ready = sem("outT_ready")
        stored = sem("stored")

        def unit_of(f, t):
            return f * NH + t

        def slot_of(f):
            return f % 2

        def shared_parts(f):
            s = slot_of(f)
            if f < SF:
                gu = [(shared_gu_lo[:, :, k, f * P:(f + 1) * P], gu_hi[:, s, :, k, :],
                       shared_gu[:, :, k, f * P:(f + 1) * P]) for k in range(KD)]
                return gu, [(shared_d_lo[:, f, :], dn_hi[:, s, :], shared_d[:, f, :])]
            gu = [(short_lo[:, :, g * SR:(g + 1) * SR], gu_hi[:, s, 0, :, g * SR:(g + 1) * SR],
                   shared_gu[:, g, :, SF * P:IS]) for g in range(2)]
            return gu, [(shared_d_lo[0:SR, SF, :], dn_hi[0:SR, s, :], shared_d[0:SR, SF, :])]

        def routed_parts(e):
            return routed_gu_lo[:, e, :, :], routed_gu_hi[:, e, :, :], routed_gu[:, e, :, :]

        def tile(j, c):
            return RING * j + c

        def lap(j, c):
            return j + c // RING

        def turn(j, c):
            return (RING // 2) * j + c // 2

        def has(i, before):
            return not isinstance(i, int) or i >= before

        def load_cond_b(engine, k):
            engine.dma_start(cond_b_sb[:, k, :, :],
                             cond_b[:, k * P:(k + 1) * P, :].rearrange("a p r -> p a r")).then_inc(cond_in, 16)

        block = ctx.enter_context(nc.Block())

        @block.sync
        def _(sp):
            for t in range(NH):
                tiles = slice(t * TPH, (t + 1) * TPH)
                sp.dma_start(x_sb[:, tiles, :], x_tok[:, tiles, :]).then_inc(x_in[t], 16)
                if t == 0:
                    sp.dma_start(cond_a_sb[:], cond_a.rearrange("a r d -> (a r) d")).then_inc(cond_in, 16)
                    load_cond_b(sp, 1)
            sp.dma_start(shw_sb[:], sh_gate_w.rearrange("(k p) o -> p k o", p=P),
                         allow_slow_non_contiguous=True).then_inc(small_in, 16)
            sp.dma_start(idx_sb[:], adapter_idx.rearrange("(a b) -> a b", a=1).to_broadcast([P, B])).then_inc(small_in, 16)
            for g, w in enumerate((sh_gate, sh_up)):
                sp.dma_start(shared_gu[:, g, :, :], w.rearrange("(k p) i -> p k i", p=P)).then_inc(shared_in, 16)
            sp.dma_start(shared_d[:, 0:SF, :],
                         sh_down[0:SF * P, :].rearrange("(c p) d -> p c d", p=P)).then_inc(shared_in, 16)
            sp.dma_start(shared_d[0:SR, SF, :], sh_down[SF * P:IS, :]).then_inc(shared_in, 16)
            for q in range(LOADS):
                es = slice(q * EL, (q + 1) * EL)
                for g, w in enumerate((w_gate, w_up)):
                    for k in range(KD):
                        sp.dma_start(routed_gu[:, es, k, g * I:(g + 1) * I],
                                     w[es, k * P:(k + 1) * P, :].rearrange("e p i -> p e i")).then_inc(routed_in[q], 16)
            sp.dma_start(routed_d[:, :, 0, :], w_down[:, 0:P, :].rearrange("e p d -> p e d")).then_inc(routed_d_in, 16)
            sp.dma_start(routed_d[0:IR, :, 1, :], w_down[:, P:I, :].rearrange("e p d -> p e d")).then_inc(routed_d_in, 16)
            sp.wait_ge(zeros_done, 1)
            sp.dma_start(h_rows[N:N + PAD, :], zeros[:]).then_inc(rows_out, 16)
            sp.dma_start(out[N:N + PAD, :], zeros[:, 0:D]).then_inc(sums_zero, 16)
            sp.dma_start(even_sums.rearrange("(n p) d -> p n d", p=P),
                         zeros[:, 0:D].unsqueeze(1).to_broadcast([P, NT + PAD // P, D])).then_inc(sums_zero, 16)
            sp.wait_ge(comb_done, 1)
            sp.wait_ge(hrow_copied, NT // 2)
            sp.dma_start(h_rows[0:N, :].rearrange("(n p) c -> p n c", p=P), h_row[:]).then_inc(rows_out, 16)
            for q in range(NT // 2):
                tk = slice(2 * q, 2 * q + 2)
                sp.wait_ge(base_done, 2 * q + 2)
                sp.dma_start(out_tok[:, tk, :], x_sb[:, tk, :]).then_inc(base_stored, 16)

        @block.gpsimd
        def _(pool):
            nc.gpsimd.memset(ident[:], 0.0).then_inc(pool_step, 1)
            pool.wait_ge(pool_step, 1)
            nc.gpsimd.affine_select(out=ident[:], in_=ident[:], compare_op=ALU.not_equal, fill=1.0, base=0,
                                    pattern=[[-1, P]], channel_multiplier=1).then_inc(ident_ready, 1)
            nc.gpsimd.memset(gates_w[:], 0.0).then_inc(gates_w_done, 1)
            nc.gpsimd.iota(part_i[:], pattern=[[0, 1]], base=0, channel_multiplier=1).then_inc(pool_step, 1)
            nc.gpsimd.iota(experts[:], pattern=[[1, E]], base=0, channel_multiplier=0,
                           allow_small_or_imprecise_dtypes=True).then_inc(pool_step, 1)
            nc.gpsimd.memset(zeros[:], 0.0).then_inc(zeros_done, 1)
            nc.gpsimd.memset(before[:], 1.0).then_inc(pool_step, 1)
            nc.gpsimd.memset(ones[:], 1.0).then_inc(pool_step, 1)
            nc.gpsimd.memset(below[:], 1.0).then_inc(pool_step, 1)
            pool.wait_ge(pool_step, 6)
            nc.gpsimd.affine_select(out=before[:], in_=before[:], compare_op=ALU.is_gt, fill=0.0, base=0,
                                    pattern=[[1, P]], channel_multiplier=-1).then_inc(pool_step, 1)
            nc.gpsimd.affine_select(out=below[:], in_=below[:], compare_op=ALU.is_gt, fill=0.0, base=0,
                                    pattern=[[1, E], [-1, E]], channel_multiplier=0).then_inc(pool_step, 1)
            nc.gpsimd.iota(lanes[:], pattern=[[1, P]], base=0, channel_multiplier=0,
                           allow_small_or_imprecise_dtypes=True).then_inc(pool_step, 1)
            nc.gpsimd.iota(tiles[:], pattern=[[1, TILES]], base=0, channel_multiplier=0,
                           allow_small_or_imprecise_dtypes=True).then_inc(pool_step, 1)
            nc.gpsimd.iota(token1[:], pattern=[[P, NT]], base=1, channel_multiplier=1,
                           allow_small_or_imprecise_dtypes=True).then_inc(pool_step, 1)
            nc.gpsimd.iota(empty1[:], pattern=[[0, 1]], base=N + 1, channel_multiplier=1,
                           allow_small_or_imprecise_dtypes=True).then_inc(pool_step, 1)

            def chunk_gate_up(f):
                pool.wait_ge(wgu_hi_done, f + 1)
                for lo, hi, raw in shared_parts(f)[0]:
                    last = nc.gpsimd.tensor_tensor(lo, raw, f32(hi), ALU.subtract)
                last.then_inc(wgu_lo_done, 1)

            def chunk_down(f):
                pool.wait_ge(wdn_hi_done, f + 1)
                for lo, hi, raw in shared_parts(f)[1]:
                    last = nc.gpsimd.tensor_tensor(lo, raw, f32(hi), ALU.subtract)
                last.then_inc(wdn_lo_done, 1)

            def tile_hots(tiles_of):
                for n in tiles_of:
                    pool.wait_ge(tile_f_done, 1)
                    for k in range(TOP_K):
                        last = nc.gpsimd.tensor_scalar(tile_hot[:, n, k, :], tiles[:], tile_f[:, n, k:k + 1],
                                                       token1[:, n:n + 1], ALU.is_equal, ALU.mult)
                    last.then_inc(tile_hot_done, 1)

            def split_low(experts_of):
                for e in experts_of:
                    lo, hi, raw = routed_parts(e)
                    pool.wait_ge(routed_hi_done, e + 1)
                    nc.gpsimd.tensor_tensor(lo, raw, f32(hi), ALU.subtract).then_inc(routed_lo_pool, 1)

            chunk_gate_up(0)
            chunk_down(0)
            split_low((1,))
            chunk_gate_up(1)
            split_low((3,))
            chunk_down(1)
            split_low((4, 5))
            chunk_gate_up(2)
            chunk_down(2)
            split_low((6, 7))
            chunk_gate_up(3)
            split_low((8,))
            chunk_down(3)
            split_low((9,))
            tile_hots((0,))
            chunk_gate_up(4)
            tile_hots((2, 4))
            chunk_down(4)
            tile_hots((6,))
            split_low((10,))
            chunk_gate_up(5)
            chunk_down(5)

            def gather(j, c):
                i, s = tile(j, c), c % RING
                pool.wait_ge(rows_out, 16 * 2)
                pool.wait_ge(gather_id_done, i + 1)
                if has(i, RING):
                    pool.wait_ge(hg_ready, i - (RING - 1))
                    pool.wait_ge(w_done, i - (RING - 1))
                pool.sem_inc(pool_clear, 1)
                nc.gpsimd.indirect_dma_start(rows[:, s, :], None, h_rows,
                                             bass.IndirectOffsetOnAxis(ap=gather_id[:, s:s + 1], axis=0)
                                             ).then_inc(rows_in[s], 16)

            def add(j, c):
                i, s, b = tile(j, c), c % RING, c % 2
                pool.wait_ge(sums_zero, 16 * 2)
                if b == 1:
                    pool.wait_ge(base_stored, 16 * (NT // 2))
                pool.wait_ge(y_copied, i + 1)
                pool.wait_ge(add_id_done, i + 1)
                if has(i, 2):
                    pool.wait_ge(added[b], turn(j, c) * 16)
                pool.sem_inc(pool_clear, 1)
                nc.gpsimd.indirect_dma_start(targets[b], bass.IndirectOffsetOnAxis(ap=add_id[:, s:s + 1], axis=0),
                                             y[:, s, :], None, compute_op=ALU.add).then_inc(added[b], 16)

            behind = 5
            for i in range(2 * RING):
                gather(0, i)
                if i == 1:
                    split_low((13, 15))
                if i >= behind:
                    add(0, i - behind)
            with pool.Fori(0, LAPS - 1) as j:
                for b in range(RING):
                    gather(j, 2 * RING + b)
                    add(j, 2 * RING + b - behind)
            for i in range(RING * (LAPS + 1), TILES):
                gather(0, i)
                add(0, i - behind)
            for i in range(TILES - behind, TILES):
                add(0, i)
            pool.wait_ge(added[1], 16 * (TILES // 2))
            pool.wait_ge(added[0], 16 * ((TILES + 1) // 2))
            nc.gpsimd.dma_start(out[0:N, :], even_sums[0:N, :], accum_op=ALU.add,
                                max_dma_last_dim=4096).then_inc(stored, 16)
            pool.wait_ge(stored, 16)

        @block.scalar
        def _(act):
            act.dma_start(cond_w_sb[:], cond_w.rearrange("(k p) d -> p k d", p=P)).then_inc(cond_in, 16)
            load_cond_b(act, 0)
            act.dma_start(router_sb[:], router_w).then_inc(cond_in, 16)
            act.dma_start(scale_sb[:], scalings.rearrange("(a o) -> a o", o=1).unsqueeze(1)
                          .to_broadcast([NA, RANK, 1]), allow_slow_non_contiguous=True).then_inc(small_in, 16)

            def x_high(t):
                for k in range(KD):
                    act.wait_ge(xT_ready, t * KD + k + 1)
                    nc.scalar.activation(xT_hi[:, k, t * HALF:(t + 1) * HALF], acc[k][t][:, :],
                                         ACT.Copy).then_inc(x_hi_done, 1)

            x_high(0)
            for j, ps in enumerate((abT_ps, wT_ps)):
                act.wait_ge(condT_ready, j + 1)
                nc.scalar.activation(condT_hi[:, 4 * j:4 * j + 4, :].rearrange("p b c -> p (b c)"), ps[:, :],
                                     ACT.Copy).then_inc(cond_hi_done, 1)
            x_high(1)
            act.wait_ge(gates_w_done, 3)
            nc.scalar.activation(gates_hi[:], gates_w[:], ACT.Copy).then_inc(gates_hi_done, 1)

            def high_parts(gu, dn):
                for _, dst, raw in gu:
                    last = nc.scalar.activation(dst, raw, ACT.Copy)
                last.then_inc(wgu_hi_done, 1)
                for _, dst, raw in dn:
                    last = nc.scalar.activation(dst, raw, ACT.Copy)
                last.then_inc(wdn_hi_done, 1)

            for t in range(NH):
                cols = slice(t * HALF, (t + 1) * HALF)
                act.wait_ge(xa_done, t + 1)
                if t:
                    act.wait_ge(h_ready, t * KD)
                nc.scalar.activation(xa_hi[:], xa[:], ACT.Copy).then_inc(xa_hi_done, 1)
                if t:
                    act.wait_ge(shared_in, 16 * 4)
                    high_parts(*shared_parts(0))
                for o in range(KD):
                    act.wait_ge(h_ready, t * KD + o + 1)
                    nc.scalar.activation(hT_hi[:, o, cols], h_ps[o][t][:, :], ACT.Copy).then_inc(h_hi_done, 1)
                for o in range(KD):
                    act.wait_ge(h_lo_done, t * KD + o + 1)
                    nc.scalar.activation(hT[:, o, cols], h_ps[o][t][:, :], ACT.Copy).then_inc(hT_done, 1)

            def copy_logits(t):
                act.wait_ge(gates_ready, t + 1)
                nc.scalar.activation(logitsT[:, t * HALF:(t + 1) * HALF], gates_ps[t][0:LG, :],
                                     ACT.Copy).then_inc(logits_copied, 1)

            def exponentials():
                act.wait_ge(tok_ready, 1)
                nc.scalar.activation(sg[:], tok_ps[:, 0:NT * LG].rearrange("p (n e) -> p n e", e=LG)[:, :, E],
                                     ACT.Tanh, scale=0.5).then_inc(tanh_done, 1)
                act.wait_ge(shifted_done, 1)
                nc.scalar.activation(expd[:], shifted[:], ACT.Exp).then_inc(exp_done, 1)

            def copy_rows():
                for q in range(NT // 2):
                    act.wait_ge(hrow_ready, q + 1)
                    nc.scalar.activation(h_row[:, 2 * q:2 * q + 2, 0:D],
                                         hrow_ps[q][:, :].rearrange("p (n d) -> p n d", d=D),
                                         ACT.Copy).then_inc(hrow_copied, 1)

            def gate_half(f, t, rows=P):
                n = unit_of(f, t)
                act.wait_ge(gate_ready if rows == P else up_ready, n + 1)
                if n >= NH:
                    act.wait_ge(down_done, n - (NH - 1))
                nc.scalar.activation(silu[0:rows, t, :], gate_ps[t][0:rows, :], ACT.Silu).then_inc(silu_done, 1)

            def high_half(f, t, rows=P):
                n = unit_of(f, t)
                act.wait_ge(inner_done, n + 1)
                nc.scalar.activation(inner_hi[0:rows, t, :], inner[0:rows, t, :],
                                     ACT.Copy).then_inc(inner_hi_done, 1)

            def split_high(experts_of):
                for e in experts_of:
                    _, hi, raw = routed_parts(e)
                    act.wait_ge(routed_in[e // EL], 16 * 2 * KD)
                    if e >= LATE:
                        act.wait_ge(rows_out, 16 * 2)
                    nc.scalar.activation(hi, raw, ACT.Copy).then_inc(routed_hi_done, 1)

            def copy_hg(j, c):
                i, b = tile(j, c), c % 2
                act.wait_ge(hg_ready, i + 1)
                if has(i, 2):
                    act.wait_ge(rgu_ready, i - 1)
                nc.scalar.activation(hg_hi[:, b, :, :].rearrange("p k s -> p (k s)"), hg_ps[b][:, 0:KD * P],
                                     ACT.Copy).then_inc(hg_hi_done, 1)

            def chunk(f, parts, rows=P):
                if f == 0:
                    copy_logits(0)
                gate_half(f, 0, rows)
                split_high(ACT_WITHIN.get((f, 0), ()))
                high_half(f, 0, rows)
                if f == 0:
                    copy_logits(1)
                if parts:
                    gu, dn = parts
                    if f > 0:
                        act.wait_ge(up_ready, unit_of(f, 0))
                    for _, dst, raw in gu:
                        last = nc.scalar.activation(dst, raw, ACT.Copy)
                    last.then_inc(wgu_hi_done, 1)
                split_high(ACT_BEHIND.get((f, 0), ()))
                gate_half(f, 1, rows)
                split_high(ACT_WITHIN.get((f, 1), ()))
                if f == 0:
                    exponentials()
                    copy_rows()
                if f == SF:
                    copy_hg(0, 0)
                if parts:
                    if f > 0:
                        act.wait_ge(down_done, unit_of(f, 0))
                    for _, dst, raw in dn:
                        last = nc.scalar.activation(dst, raw, ACT.Copy)
                    last.then_inc(wdn_hi_done, 1)
                high_half(f, 1, rows)
                split_high(ACT_BEHIND.get((f, 1), ()))

            for f in range(SHARED):
                chunk(f, shared_parts(f + 1) if f + 1 < SHARED else None, P if f < SF else SR)
            for t in range(NH):
                act.wait_ge(down_done, unit_of(SHARED - 1, t) + 1)
                nc.scalar.activation(sharedT[:, 0, t * HALF:(t + 1) * HALF], acc[0][t][:, :],
                                     ACT.Copy).then_inc(accT_a, 1)
                if t == 0:
                    copy_hg(0, 1)

            def silu_tile(j, c):
                i, b = tile(j, c), c % 2
                act.wait_ge(rgu_ready, i + 1)
                if has(i, 2):
                    act.wait_ge(r_inner_done, i - 1)
                nc.scalar.activation(r_silu[:, b, :], rgu_ps[b][:, 0:I], ACT.Silu).then_inc(r_silu_done, 1)

            def copy_y(j, c):
                i, s, b = tile(j, c), c % RING, c % 2
                act.wait_ge(y_ready, i + 1)
                if has(i, RING):
                    act.wait_ge(added[b], (turn(j, c) - (RING // 2 - 1)) * 16)
                nc.scalar.activation(y[:, s, :], y_ps[b][:, 0:D], ACT.Copy).then_inc(y_copied, 1)

            def copy_innerT(j, c):
                i, b = tile(j, c), c % 2
                act.wait_ge(innerT_ready, i + 1)
                if has(i, 2):
                    act.wait_ge(y_ready, i - 1)
                nc.scalar.activation(innerT[:, b, 0, :], innerT_ps[b][:, 0:P], ACT.Copy)
                nc.scalar.activation(innerT[0:IR, b, 1, :], innerT_ps[b][0:IR, P:2 * P],
                                     ACT.Copy).then_inc(innerT_copied, 1)

            for i in range(4):
                if i >= 1:
                    copy_hg(0, i + 1)
                silu_tile(0, i)
                if i >= 2:
                    copy_y(0, i - 2)
                if i >= 1:
                    copy_innerT(0, i - 1)
            with act.Fori(0, LAPS) as j:
                for c in range(4, 4 + RING):
                    copy_hg(j, c + 1)
                    silu_tile(j, c)
                    copy_y(j, c - 2)
                    copy_innerT(j, c - 1)
            for i in range(TILES - 3, TILES):
                if i + 1 < TILES:
                    copy_hg(0, i + 1)
                silu_tile(0, i)
                copy_y(0, i - 2)
                copy_innerT(0, i - 1)
            copy_y(0, TILES - 2)
            copy_innerT(0, TILES - 1)
            copy_y(0, TILES - 1)

        @block.vector
        def _(dve):
            steps = [0]

            def step(ins):
                steps[0] += 1
                ins.then_inc(dve_step, 1)
                dve.wait_ge(dve_step, steps[0])

            def x_low(t):
                for k in range(KD):
                    cols = slice(t * HALF, (t + 1) * HALF)
                    dve.wait_ge(x_hi_done, t * KD + k + 1)
                    nc.vector.tensor_tensor(xT_lo[:, k, cols], acc[k][t][:, :], xT_hi[:, k, cols].bitcast(F32),
                                            ALU.subtract).then_inc(x_lo_done, 1)

            x_low(0)
            for j, ps in enumerate((abT_ps, wT_ps)):
                dve.wait_ge(cond_hi_done, j + 1)
                blocks = slice(4 * j, 4 * j + 4)
                nc.vector.tensor_tensor(condT_lo[:, blocks, :].rearrange("p b c -> p (b c)"), ps[:, :],
                                        condT_hi[:, blocks, :].rearrange("p b c -> p (b c)").bitcast(F32),
                                        ALU.subtract).then_inc(cond_lo_done, 1)
                if j == 0:
                    dve.wait_ge(routerT_ready, 1)
                    dve.wait_ge(gates_w_done, 1)
                    nc.vector.tensor_copy(gates_w[:, :, 0:E], routerT_ps[:, 0:KD * E]
                                          .rearrange("p (k e) -> p k e", e=E)).then_inc(gates_w_done, 1)
            dve.wait_ge(small_in, 16 * 3)
            nc.vector.tensor_copy(gates_w[:, :, E:E + 1], shw_sb[:]).then_inc(gates_w_done, 1)
            dve.wait_ge(pool_step, 3)
            step(nc.vector.tensor_single_scalar(part_a[:], part_i[:], RANK.bit_length() - 1, ALU.arith_shift_right))
            step(nc.vector.tensor_copy(adapter_of_part[:], part_a[:]))
            step(nc.vector.tensor_copy(idx_f[:], idx_sb[:]))
            step(nc.vector.tensor_scalar(adapter_coef[:], idx_f[:], adapter_of_part[:, 0:1], scale_sb[:, 0:1],
                                         ALU.is_equal, ALU.mult))
            for t in range(NH):
                dve.wait_ge(xa_ready, t + 1)
                if t:
                    dve.wait_ge(xa_lo_done, t)
                    dve.wait_ge(xa_hi_done, t)
                nc.vector.tensor_tensor(
                    xa[:].rearrange("p (b t) -> p b t", t=T), xa_ps[t][:, :].rearrange("p (b t) -> p b t", t=T),
                    adapter_coef[:, t * BH:(t + 1) * BH].unsqueeze(2).to_broadcast([P, BH, T]),
                    ALU.mult).then_inc(xa_done, 1)
                dve.wait_ge(xa_hi_done, t + 1)
                nc.vector.tensor_tensor(xa_lo[:], xa[:], xa_hi[:].bitcast(F32), ALU.subtract).then_inc(xa_lo_done, 1)
                if t == 0:
                    x_low(1)
                    dve.wait_ge(gates_hi_done, 1)
                    nc.vector.tensor_tensor(gates_lo[:], gates_w[:], gates_hi[:].bitcast(F32),
                                            ALU.subtract).then_inc(gates_lo_done, 1)
                for o in range(KD):
                    cols = slice(t * HALF, (t + 1) * HALF)
                    dve.wait_ge(h_hi_done, t * KD + o + 1)
                    nc.vector.tensor_tensor(hT_lo[:, o, cols], h_ps[o][t][:, :], hT_hi[:, o, cols].bitcast(F32),
                                            ALU.subtract).then_inc(h_lo_done, 1)
            def over_experts(v):
                return v[:].unsqueeze(2).to_broadcast([P, NT, E])

            def softmax():
                tok = tok_ps[:, 0:NT * LG].rearrange("p (n e) -> p n e", e=LG)[:, :, 0:E]
                dve.wait_ge(tok_ready, 1)
                dve.wait_ge(tanh_done, 1)
                step(nc.vector.tensor_reduce(mx[:], tok, AX_X, ALU.max))
                nc.vector.tensor_tensor(shifted[:], tok, over_experts(mx), ALU.subtract).then_inc(shifted_done, 1)
                nc.vector.tensor_scalar(sg[:], sg[:], 0.5, 0.5, ALU.mult, ALU.add).then_inc(sg_done, 1)
                dve.wait_ge(exp_done, 1)
                step(nc.vector.tensor_reduce(den[:], expd[:], AX_X, ALU.add))
                step(nc.vector.reciprocal(rden[:], den[:]))
                step(nc.vector.tensor_tensor(probs[:], expd[:], over_experts(rden), ALU.mult))

            def multiply(f, t, rows=P, up_src=None):
                n = unit_of(f, t)
                dve.wait_ge(up_ready, n + 1)
                dve.wait_ge(silu_done, n + 1)
                nc.vector.tensor_tensor(inner[0:rows, t, :], up_ps[t][:, :] if up_src is None else up_src,
                                        silu[0:rows, t, :], ALU.mult).then_inc(inner_done, 1)

            def low_part(f, t, rows=P):
                n = unit_of(f, t)
                dve.wait_ge(inner_hi_done, n + 1)
                nc.vector.tensor_tensor(inner_lo[0:rows, t, :], inner[0:rows, t, :],
                                        f32(inner_hi[0:rows, t, :]),
                                        ALU.subtract).then_inc(inner_lo_done, 1)

            def choose():
                for n in range(NT):
                    last = nc.vector.max(top[:, n, :], probs[:, n, :])
                step(last)
                for n in range(NT):
                    last = nc.vector.max_index(top_i[:, n, :], top[:, n, :], probs[:, n, :])
                step(last)

            def weigh():
                step(nc.vector.tensor_copy(top_f[:], top_i[:]))
                step(nc.vector.tensor_tensor(
                    hit[:], experts[:].unsqueeze(1).unsqueeze(1).to_broadcast([P, NT, TOP_K, E]),
                    top_f[:, :, 0:TOP_K].unsqueeze(3).to_broadcast([P, NT, TOP_K, E]), ALU.is_equal))
                step(nc.vector.tensor_reduce(picked[:], hit[:].rearrange("p n k e -> p n e k"), AX_X, ALU.add))
                nc.vector.tensor_copy(picked_b[:], picked[:]).then_inc(picked_done, 1)
                step(nc.vector.tensor_reduce(topsum[:], top[:, :, 0:TOP_K], AX_X, ALU.add))
                step(nc.vector.tensor_scalar(topsum[:], topsum[:], 1e-9, None, ALU.max))
                step(nc.vector.reciprocal(rtop[:], topsum[:]))
                step(nc.vector.tensor_tensor(kept[:], picked[:], probs[:], ALU.mult))
                nc.vector.tensor_tensor(h_row[:, :, D:ROW], kept[:], over_experts(rtop), ALU.mult).then_inc(comb_done, 1)

            def take_counts():
                dve.wait_ge(count_ready, 1)
                nc.vector.tensor_copy(counts[:], count_ps[:, 0:NT * E + E]).then_inc(count_copied, 1)
                dve.wait_ge(count_copied, 1)

            def place_experts():
                step(nc.vector.tensor_scalar(tiles_i[:], counts[:, NT * E:], float(P - 1), None, ALU.add))
                step(nc.vector.tensor_single_scalar(tiles_s[:], tiles_i[:], P.bit_length() - 1, ALU.arith_shift_right))
                step(nc.vector.tensor_copy(tiles_f[:], tiles_s[:]))
                dve.wait_ge(pool_step, 8)
                step(nc.vector.tensor_tensor(below[:], below[:], tiles_f[:].unsqueeze(1).to_broadcast([P, E, E]),
                                             ALU.mult))
                step(nc.vector.tensor_reduce(begin[:], below[:], AX_X, ALU.add))
                step(nc.vector.tensor_tensor(end[:], begin[:], tiles_f[:], ALU.add))
                step(nc.vector.scalar_tensor_tensor(
                    out=slot_e[:], in0=begin[:].unsqueeze(1).to_broadcast([P, NT, E]), scalar=float(P),
                    in1=counts[:, 0:NT * E].rearrange("p (n e) -> p n e", e=E), op0=ALU.mult, op1=ALU.add))

            def place_pairs():
                step(nc.vector.tensor_tensor(hit[:], hit[:],
                                             slot_e[:].unsqueeze(2).to_broadcast([P, NT, TOP_K, E]), ALU.mult))
                step(nc.vector.tensor_reduce(slot_k[:], hit[:], AX_X, ALU.add))
                step(nc.vector.tensor_copy(slot_i[:], slot_k[:]))
                step(nc.vector.tensor_single_scalar(lane_i[:], slot_i[:], P - 1, ALU.bitwise_and))
                step(nc.vector.tensor_single_scalar(tile_i[:], slot_i[:], P.bit_length() - 1, ALU.arith_shift_right))
                nc.vector.tensor_copy(tile_f[:], tile_i[:]).then_inc(tile_f_done, 1)
                step(nc.vector.tensor_copy(lane_f[:], lane_i[:]))

            def one_hot(n):
                dve.wait_ge(pool_step, 12)
                for k in range(TOP_K):
                    last = nc.vector.tensor_scalar(lane_hot[:, n, k, :], lanes[:], lane_f[:, n, k:k + 1], None,
                                                   ALU.is_equal)
                    if n % 2:
                        last = nc.vector.tensor_scalar(tile_hot[:, n, k, :], tiles[:], tile_f[:, n, k:k + 1],
                                                       token1[:, n:n + 1], ALU.is_equal, ALU.mult)
                last.then_inc(hot_done, 1)

            def take_tokens():
                dve.wait_ge(token_ready, 1)
                step(nc.vector.tensor_scalar(vacant[:], token_ps[:, 0:TILES], 0.0, empty1[:, 0:1],
                                             ALU.is_equal, ALU.mult))
                nc.vector.scalar_tensor_tensor(out=slot_token[:], in0=token_ps[:, 0:TILES], scalar=-1.0,
                                               in1=vacant[:], op0=ALU.add, op1=ALU.add).then_inc(token_done, 1)
                dve.wait_ge(token_done, 1)
                for i in range(RING):
                    nc.vector.tensor_copy(gather_id[:, i:i + 1], slot_token[:, i:i + 1]).then_inc(gather_id_done, 1)

            def ended_experts():
                nc.vector.tensor_tensor(ended[:], tiles[:].unsqueeze(2).to_broadcast([P, TILES, E]),
                                        end[:].unsqueeze(1).to_broadcast([P, TILES, E]), ALU.is_ge).then_inc(ended_done, 1)

            def place_tiles():
                dve.wait_ge(ended_done, 1)
                step(nc.vector.tensor_reduce(expert_f[:], ended[:], AX_X, ALU.add))
                nc.vector.tensor_scalar(expert_of[:], expert_f[0:1, :], float(E - 1), None, ALU.min).then_inc(expert_done, 1)

            def mark_tiles():
                step(nc.vector.tensor_tensor(tile_expert[:], experts[:].unsqueeze(1).to_broadcast([P, TILES, E]),
                                             expert_f[:].unsqueeze(2).to_broadcast([P, TILES, E]), ALU.is_equal))

            def split_low(experts_of):
                for e in experts_of:
                    lo, hi, raw = routed_parts(e)
                    dve.wait_ge(routed_hi_done, e + 1)
                    nc.vector.tensor_tensor(lo, raw, f32(hi), ALU.subtract).then_inc(routed_lo_dve, 1)

            def low_hg(j, c):
                i, b = tile(j, c), c % 2
                dve.wait_ge(hg_hi_done, i + 1)
                nc.vector.tensor_tensor(hg_lo[:, b, :, :].rearrange("p k s -> p (k s)"), hg_ps[b][:, 0:KD * P],
                                        f32(hg_hi[:, b, :, :]).rearrange("p k s -> p (k s)"),
                                        ALU.subtract).then_inc(hg_lo_done, 1)

            ahead_of = {(SF, 1): [lambda: low_hg(0, 0)]}
            between = {(0, 1): [softmax], (2, 0): [take_counts], (4, 1): [take_tokens], (SF, 1): [mark_tiles]}
            behind = {(0, 1): [choose], (1, 0): [weigh], (2, 0): [place_experts], (2, 1): [place_pairs],
                      (4, 1): [ended_experts], (5, 0): [place_tiles]}
            lanes_between = {(3, 0): (0,), (3, 1): (3,), (4, 0): (6, 7)}
            lanes_behind = {(3, 0): (1, 2), (3, 1): (4, 5)}
            for f in range(SHARED):
                for t in range(NH):
                    for work in ahead_of.get((f, t), ()):
                        work()
                    if f < SF:
                        multiply(f, t)
                    else:
                        multiply(f, t, SR, gate_ps[t][SR:2 * SR, :])
                    for work in between.get((f, t), ()):
                        work()
                    for n in lanes_between.get((f, t), ()):
                        one_hot(n)
                    split_low(DVE_WITHIN.get((f, t), ()))
                    low_part(f, t, P if f < SF else SR)
                    for n in lanes_behind.get((f, t), ()):
                        one_hot(n)
                    split_low(DVE_BEHIND.get((f, t), ()))
                    for work in behind.get((f, t), ()):
                        work()

            def take_shared(t):
                dve.wait_ge(down_done, unit_of(SHARED - 1, t) + 1)
                nc.vector.tensor_copy(sharedT[:, 1, t * HALF:(t + 1) * HALF], acc[1][t][:, :]).then_inc(accT_v, 1)

            def add_shared(q):
                dve.wait_ge(sg_done, 1)
                dve.wait_ge(outT_ready, q + 1)
                for n in (2 * q, 2 * q + 1):
                    nc.vector.scalar_tensor_tensor(out=x_sb[:, n, :], in0=hrow_ps[q][:, n % 2 * D:(n % 2 + 1) * D],
                                                   scalar=sg[:, n:n + 1], in1=x_sb[:, n, :], op0=ALU.mult,
                                                   op1=ALU.add).then_inc(base_done, 1)

            def weight_slots(j, c):
                i, s, b = tile(j, c), c % RING, c % 2
                dve.wait_ge(rows_in[s], lap(j, c) * 16 + 16)
                nc.vector.tensor_tensor(w_e[:, b, :], rows[:, s, D:ROW],
                                        tile_expert[:, bass.ds(i, 1), :].rearrange("p o e -> p (o e)"),
                                        ALU.mult).then_inc(w_part, 1)
                dve.wait_ge(w_part, i + 1)
                nc.vector.tensor_reduce(w_slot[:, s:s + 1], w_e[:, b, :], AX_X, ALU.add).then_inc(w_done, 1)

            def inner_tile(j, c):
                i, s, b = tile(j, c), c % RING, c % 2
                dve.wait_ge(w_done, i + 1)
                dve.wait_ge(r_silu_done, i + 1)
                if has(i, 2):
                    dve.wait_ge(innerT_ready, i - 1)
                nc.vector.scalar_tensor_tensor(out=r_inner[:, b, :], in0=rgu_ps[b][:, I:2 * I],
                                               scalar=w_slot[:, s:s + 1], in1=r_silu[:, b, :],
                                               op0=ALU.mult, op1=ALU.mult).then_inc(r_inner_done, 1)

            def next_gather(j, c):
                i, s = tile(j, c), c % RING
                dve.wait_ge(rows_in[s], lap(j, c) * 16)
                nc.vector.tensor_copy(gather_id[:, s:s + 1], slot_token[:, bass.ds(i, 1)]).then_inc(gather_id_done, 1)

            def next_add(j, c):
                i, s, b = tile(j, c), c % RING, c % 2
                if has(i, RING):
                    dve.wait_ge(added[b], (turn(j, c) - (RING // 2 - 1)) * 16)
                nc.vector.tensor_copy(add_id[:, s:s + 1], slot_token[:, bass.ds(i, 1)]).then_inc(add_id_done, 1)

            def ahead(j, c, following=True):
                weight_slots(j, c)
                if following:
                    next_gather(j, c + RING)

            ahead(0, 0)
            take_shared(0)
            ahead(0, 1)
            low_hg(0, 1)
            take_shared(1)
            add_shared(0)
            inner_tile(0, 0)
            add_shared(1)
            add_shared(2)
            low_hg(0, 2)
            add_shared(3)
            inner_tile(0, 1)
            for i in range(2):
                next_add(0, i)
            ahead(0, 2)
            for i in range(2, 4):
                low_hg(0, i + 1)
                inner_tile(0, i)
                next_add(0, i)
                ahead(0, i + 1)
            with dve.Fori(0, LAPS - 1) as j:
                for c in range(4, 4 + RING):
                    low_hg(j, c + 1)
                    inner_tile(j, c)
                    next_add(j, c)
                    ahead(j, c + 1)
            for i in range(RING * LAPS, TILES):
                if i + 1 < TILES:
                    low_hg(0, i + 1)
                inner_tile(0, i)
                next_add(0, i)
                if i + 1 < TILES:
                    ahead(0, i + 1, i + 1 + RING < TILES)

        @block.tensor
        def _(pe):
            ALL = ("hi hi", "hi lo", "lo hi")

            def product(dst, pairs, parts=ALL, first=True, last=True, begun=None):
                terms = [(w_lo if part == "lo hi" else w_hi, m_lo if part == "hi lo" else m_hi)
                         for part in parts for w_hi, w_lo, m_hi, m_lo in pairs]
                for j, (w, m) in enumerate(terms):
                    mm = nc.tensor.matmul(dst, w, m, start=first and j == 0, stop=last and j == len(terms) - 1)
                    if j == 0 and begun is not None:
                        mm.then_inc(begun, 1)
                return mm

            pe.wait_ge(ident_ready, 1)
            for _ in range(WARM):
                nc.tensor.matmul(up_ps[1][:, 0:P], ident[:], ident[:], start=True, stop=True)

            def transpose_x(t):
                pe.wait_ge(x_in[t], 16)
                for k in range(KD):
                    for j in range(TPH):
                        mm = nc.tensor.transpose(acc[k][t][:, j * P:(j + 1) * P],
                                                 x_sb[:, t * TPH + j, k * P:(k + 1) * P], ident[:])
                    mm.then_inc(xT_ready, 1)

            transpose_x(0)
            pe.wait_ge(cond_in, 16 * (3 + KD))
            for k in range(KD):
                nc.tensor.transpose(abT_ps[:, k * P:(k + 1) * P], cond_a_sb[:, k * P:(k + 1) * P], ident[:])
            for o in range(KD):
                mm = nc.tensor.transpose(abT_ps[:, (KD + o) * P:(KD + o + 1) * P],
                                         cond_b_sb[:, o, :, :].rearrange("p a r -> p (a r)"), ident[:])
            mm.then_inc(condT_ready, 1)
            for k in range(KD):
                for o in range(KD):
                    mm = nc.tensor.transpose(wT_ps[:, (KD * k + o) * P:(KD * k + o + 1) * P],
                                             cond_w_sb[:, o, k * P:(k + 1) * P], ident[:])
            mm.then_inc(condT_ready, 1)
            for k in range(KD):
                mm = nc.tensor.transpose(routerT_ps[:, k * E:(k + 1) * E], router_sb[:, k * P:(k + 1) * P],
                                         ident[0:E, 0:E])
            mm.then_inc(routerT_ready, 1)
            transpose_x(1)

            def w_block(k, o):
                return condT_hi[:, 4 + KD * k + o, :], condT_lo[:, 4 + KD * k + o, :]

            def a_block(k):
                return condT_hi[:, k, :], condT_lo[:, k, :]

            def b_block(o):
                return condT_hi[:, KD + o, :], condT_lo[:, KD + o, :]

            for t in range(NH):
                cols = slice(t * HALF, (t + 1) * HALF)
                a_x = [(*a_block(k), xT_hi[:, k, cols], xT_lo[:, k, cols]) for k in range(KD)]
                pe.wait_ge(cond_hi_done, 1)
                pe.wait_ge(x_hi_done, (t + 1) * KD)
                if t:
                    pe.wait_ge(gates_w_done, 2)
                product(xa_ps[t][:, :], a_x, ("hi hi",), last=False)
                pe.wait_ge(x_lo_done, (t + 1) * KD)
                product(xa_ps[t][:, :], a_x, ("hi lo",), first=False, last=False)
                pe.wait_ge(cond_lo_done, 1)
                product(xa_ps[t][:, :], a_x, ("lo hi",), first=False).then_inc(xa_ready, 1)
                pe.wait_ge(cond_lo_done, 2)
                for o in range(KD):
                    product(h_ps[o][t][:, :], [(*w_block(k, o), xT_hi[:, k, cols], xT_lo[:, k, cols])
                                               for k in range(KD)], last=False)
                b_xa = [[(*b_block(o), xa_hi[:], xa_lo[:])] for o in range(KD)]
                pe.wait_ge(xa_hi_done, t + 1)
                for o in range(KD):
                    product(h_ps[o][t][:, :], b_xa[o], ("hi hi", "lo hi"), first=False, last=False)
                pe.wait_ge(xa_lo_done, t + 1)
                for o in range(KD):
                    product(h_ps[o][t][:, :], b_xa[o], ("hi lo",), first=False).then_inc(h_ready, 1)

            def gates(t):
                pe.wait_ge(gates_lo_done, 1)
                pe.wait_ge(h_lo_done, (t + 1) * KD)
                pe.wait_ge(hT_done, t * KD + 1)
                cols = slice(t * HALF, (t + 1) * HALF)
                product(gates_ps[t][0:LG, :],
                        [(gates_hi[:, k, :], gates_lo[:, k, :], hT_hi[:, k, cols], hT_lo[:, k, cols])
                         for k in range(KD)]).then_inc(gates_ready, 1)

            def transpose_logits():
                pe.wait_ge(logits_copied, NH)
                pe.wait_ge(hT_done, KD)
                for n in range(NT):
                    mm = nc.tensor.transpose(tok_ps[:, n * LG:(n + 1) * LG], logitsT[:, n * P:(n + 1) * P],
                                             ident[0:LG, 0:LG])
                mm.then_inc(tok_ready, 1)

            def transpose_h():
                for q in range(NT // 2):
                    if q == NT // 2 - 1:
                        pe.wait_ge(shifted_done, 1)
                    for j in range(2):
                        for k in range(KD):
                            mm = nc.tensor.transpose(hrow_ps[q][:, (j * KD + k) * P:(j * KD + k + 1) * P],
                                                     hT[:, k, (2 * q + j) * P:(2 * q + j + 1) * P], ident[:])
                    mm.then_inc(hrow_ready, 1)

            def gate_up(f, t, s, short=False):
                n = unit_of(f, t)
                cols = slice(t * HALF, (t + 1) * HALF)
                if t == 0:
                    pe.wait_ge(wgu_lo_done, f + 1)

                def operands(g):
                    return [(gu_hi[:, s, g, k, :],
                             short_lo[:, k, :] if short else shared_gu_lo[:, g, k, f * P:(f + 1) * P],
                             hT_hi[:, k, cols], hT_lo[:, k, cols]) for k in range(KD)]
                if n >= NH:
                    pe.wait_ge(inner_done, n - (NH - 1))
                if n < NH:
                    pe.wait_ge(xa_done, n + 1)
                if short:
                    product(gate_ps[t][:, :], operands(0), begun=gate_ready).then_inc(up_ready, 1)
                    return
                product(gate_ps[t][:, :], operands(0)).then_inc(gate_ready, 1)
                product(up_ps[t][:, :], operands(1)).then_inc(up_ready, 1)

            def down(f, t, s, first=False, last=False, rows=P):
                n = unit_of(f, t)
                if t == 0:
                    pe.wait_ge(wdn_lo_done, f + 1)
                terms = [[(dn_hi[0:rows, s, o * P:(o + 1) * P], shared_d_lo[0:rows, f, o * P:(o + 1) * P],
                           inner_hi[0:rows, t, :], inner_lo[0:rows, t, :])] for o in range(KD)]
                pe.wait_ge(inner_hi_done, n + 1)
                for o in range(KD):
                    product(acc[o][t][:, :], terms[o], ("hi hi", "lo hi"), first=first, last=False)
                pe.wait_ge(inner_lo_done, n + 1)
                for o in range(KD):
                    mm = product(acc[o][t][:, :], terms[o], ("hi lo",), first=False, last=last)
                mm.then_inc(down_done, 1)

            def count():
                pe.wait_ge(picked_done, 1)
                pe.wait_ge(pool_step, 8)
                for n in range(NT - 1):
                    behind = NT - 1 - n
                    nc.tensor.matmul(count_ps[:, (n + 1) * E:NT * E], ones[:],
                                     picked_b[:, n:n + 1, :].to_broadcast([P, behind, E]),
                                     start=n == 0, stop=False, skip_group_check=True)
                nc.tensor.matmul(count_ps[:, 0:NT * E], before[:], picked_b[:].rearrange("p n e -> p (n e)"),
                                 start=False, stop=True, skip_group_check=True)
                for n in range(NT):
                    mm = nc.tensor.matmul(count_ps[:, NT * E:NT * E + E], ones[:], picked_b[:, n, :],
                                          start=n == 0, stop=n == NT - 1, skip_group_check=True)
                mm.then_inc(count_ready, 1)

            def tabulate():
                for n in range(NT):
                    pe.wait_ge(hot_done, n + 1)
                    if n % 2 == 0:
                        pe.wait_ge(tile_hot_done, n // 2 + 1)
                    for k in range(TOP_K):
                        mm = nc.tensor.matmul(token_ps[:, 0:TILES], lane_hot[:, n, k, :], tile_hot[:, n, k, :],
                                              start=n == 0 and k == 0, stop=n == NT - 1 and k == TOP_K - 1)
                mm.then_inc(token_ready, 1)

            gates(0)
            gate_up(0, 0, slot_of(0))
            gates(1)
            gate_up(0, 1, slot_of(0))
            transpose_logits()
            pe.wait_ge(hT_done, NH * KD)
            transpose_h()
            for f in range(1, SHARED):
                short = f == SF
                rows_f = SR if short else P
                if f == SF:
                    pe.wait_ge(token_done, 1)
                gate_up(f, 0, slot_of(f), short)
                if f == 2:
                    pe.wait_ge(inner_done, unit_of(f, 0))
                    count()
                if f == 1:
                    pe.wait_ge(hrow_copied, NT // 2)
                    down(0, 0, slot_of(0), first=True)
                down(f - 1, 1, slot_of(f - 1), first=f == 1)
                if f == 2:
                    pe.wait_ge(count_copied, 1)
                gate_up(f, 1, slot_of(f), short)
                if f == SF - 1:
                    pe.wait_ge(inner_done, unit_of(f, 0) + 1)
                    tabulate()
                if not short:
                    down(f, 0, slot_of(f))

            def transpose_shared():
                for q in range(NT // 2):
                    pe.wait_ge(accT_a, q // 2 + 1)
                    pe.wait_ge(accT_v, q // 2 + 1)
                    if q == 1:
                        pe.wait_ge(accT_a, NH)
                    for j in range(2):
                        n = 2 * q + j
                        for k in range(KD):
                            mm = nc.tensor.transpose(hrow_ps[q][:, (j * KD + k) * P:(j * KD + k + 1) * P],
                                                     sharedT[:, k, n * P:(n + 1) * P], ident[:])
                    mm.then_inc(outT_ready, 1)

            def transpose_rows(j, c):
                i, s, b = tile(j, c), c % RING, c % 2
                pe.wait_ge(rows_in[s], lap(j, c) * 16 + 16)
                for k in range(KD):
                    mm = nc.tensor.transpose(hg_ps[b][:, k * P:(k + 1) * P], rows[:, s, k * P:(k + 1) * P], ident[:])
                mm.then_inc(hg_ready, 1)

            def expert(i):
                return pe.value_load(expert_of[0:1, bass.ds(i, 1)], min_val=0, max_val=E - 1)

            def experts_of_lap(j):
                _, values = nc.values_load_multi_w_load_instructions(
                    expert_of[0:1, bass.ds(RING * j, 2 * RING)], engines=(mybir.EngineType.PE,),
                    min_val=0, max_val=E - 1, skip_runtime_bounds_check_because="place_tiles keeps them below E")
                return values

            def gate_up_tile(j, c, e):
                i, b = tile(j, c), c % 2
                pe.wait_ge(hg_hi_done, i + 1)
                if isinstance(i, int) and i == 0:
                    pe.wait_ge(routed_lo_pool, POOL_LOWS)
                    pe.wait_ge(routed_lo_dve, DVE_LOWS)
                if isinstance(i, int) and i < 2:
                    pe.wait_ge(inner_done, unit_of(SF, i) + 1)
                terms = [(h, w, k) for h, w in ((hg_hi, routed_gu_hi), (hg_hi, routed_gu_lo), (hg_lo, routed_gu_hi))
                         for k in range(KD)]
                for n, (h, w, k) in enumerate(terms):
                    if n == 2 * KD:
                        pe.wait_ge(hg_lo_done, i + 1)
                    mm = nc.tensor.matmul(rgu_ps[b][:, 0:2 * I], h[:, b, k, :],
                                          w[:, bass.ds(e, 1), k, :].rearrange("p o c -> p (o c)"),
                                          start=n == 0, stop=n == len(terms) - 1)
                mm.then_inc(rgu_ready, 1)

            def transpose_inner(j, c):
                i, b = tile(j, c), c % 2
                pe.wait_ge(r_inner_done, i + 1)
                if isinstance(i, int) and i < 2:
                    pe.wait_ge(base_done, 2 * i + 2)
                nc.tensor.transpose(innerT_ps[b][:, 0:P], r_inner[:, b, 0:P], ident[:])
                nc.tensor.transpose(innerT_ps[b][0:IR, P:2 * P], r_inner[:, b, P:I],
                                    ident[:]).then_inc(innerT_ready, 1)

            def down_tile(j, c, e):
                i, b = tile(j, c), c % 2
                pe.wait_ge(innerT_copied, i + 1)
                if has(i, 2):
                    pe.wait_ge(y_copied, i - 1)
                else:
                    pe.wait_ge(base_done, NT)
                for q, rows_q in enumerate((P, IR)):
                    w = routed_d[0:rows_q, bass.ds(e, 1), q, :].rearrange("p o d -> p (o d)")
                    mm = nc.tensor.matmul(y_ps[b][:, 0:D], innerT[0:rows_q, b, q, :], w, start=q == 0, stop=q == 1)
                mm.then_inc(y_ready, 1)

            pe.wait_ge(routed_d_in, 16 * 2)
            transpose_rows(0, 0)
            down(SF, 0, slot_of(SF), last=True, rows=SR)
            transpose_rows(0, 1)
            pe.wait_ge(expert_done, 1)
            gate_up_tile(0, 0, expert(0))
            down(SF, 1, slot_of(SF), last=True, rows=SR)
            transpose_shared()
            for i in range(1, 4):
                transpose_rows(0, i + 1)
                gate_up_tile(0, i, expert(i))
                if i >= 2:
                    down_tile(0, i - 2, expert(i - 2))
                transpose_inner(0, i - 1)
            with pe.Fori(0, LAPS) as j:
                e = experts_of_lap(j)
                for c in range(4, 4 + RING):
                    transpose_rows(j, c + 1)
                    gate_up_tile(j, c, e[c])
                    down_tile(j, c - 2, e[c - 2])
                    transpose_inner(j, c - 1)
            for i in range(TILES - 3, TILES):
                if i + 1 < TILES:
                    transpose_rows(0, i + 1)
                gate_up_tile(0, i, expert(i))
                down_tile(0, i - 2, expert(i - 2))
                transpose_inner(0, i - 1)
            down_tile(0, TILES - 2, expert(TILES - 2))
            transpose_inner(0, TILES - 1)
            down_tile(0, TILES - 1, expert(TILES - 1))


_INS = ['x', 'itok_B_0_6', 'L0_cond_W', 'L0_cond_A', 'L0_cond_Bm', 'L0_cond_scalings', 'L0_ffn_router_w',
        'L0_ffn_w_gate', 'L0_ffn_w_up', 'L0_ffn_w_down', 'L0_ffn_sh_gate', 'L0_ffn_sh_up', 'L0_ffn_sh_down',
        'L0_ffn_sh_gate_w']


def kernel(**inputs):
    import numpy as _np
    import concourse.bacc as _bacc
    from concourse import mybir as _mybir
    from concourse.bass_utils import run_bass_kernel_spmd as _run

    nc = _bacc.Bacc("TRN2", target_bir_lowering=False, num_devices=1)
    arrays, args = {}, []
    for name in _INS:
        a = _np.ascontiguousarray(inputs[name])
        arrays[f"in_{name}_dram"] = a
        args.append(nc.dram_tensor(f"in_{name}_dram", a.shape, _mybir.dt.from_np(a.dtype), kind="ExternalInput").ap())
    B, T, D = inputs["x"].shape
    out = nc.dram_tensor("out_0_dram", (B * T + P, D), _mybir.dt.float32, kind="ExternalOutput").ap()
    adaln_moe_ffn(nc, *args, out)
    r = _run(nc, [arrays], core_ids=[0])
    return r.results[0]["out_0_dram"][0:B * T].reshape(B, T, D)
```
